# Optimizing a Trainium2 kernel written in Bass

```python
import numpy as np
import jax
import jax.numpy as jnp

def _softmax(x, axis=-1):
    return jax.nn.softmax(x, axis=axis)

def _gelu(x):
    return jax.nn.gelu(x, approximate=True)

def _silu(x):
    return jax.nn.silu(x)

def _sigmoid(x):
    return jax.nn.sigmoid(x)

def _layernorm(x, axis=-1, eps=1e-05):
    m = jnp.mean(x, axis=axis, keepdims=True)
    v = jnp.var(x, axis=axis, keepdims=True)
    return (x - m) / jnp.sqrt(v + eps)

def _scatter_add(tgt, idx, src, axis=0):
    return tgt.at[idx].add(src)

def _segment_sum(src, seg, n):
    return jax.ops.segment_sum(src, seg, n)
kernel_name = 'mk_adj_seq_d4_adj_r2_8ef9cc'

def setup_inputs(seed: int=0):
    np.random.seed(seed)
    _w = jnp.asarray

    def _rec_inputs():
        import jax
        import jax.numpy as jnp
        _gk = jax.random.key(seed)
        x = -0.0002928 + 1 * jax.random.normal(jax.random.fold_in(_gk, 1), (64, 128, 256), jnp.float32)
        _a = jax.random.bernoulli(jax.random.fold_in(_gk, 2), 0.125, (64, 128, 128))
        adj = _a.astype(jnp.int32)
        return (x, adj)
    x, adj = _rec_inputs()

    def _L0_gnn_setup():
        import jax, jax.numpy as jnp
        import numpy as np
        HIDDEN = 256
        NHEADS = 8
        ALPHA = 0.1
        NUM_HOP = 4
        MASK_VAL = -16384.0
        LN_EPS = 1e-05
        key = jax.random.key(seed)
        ks = jax.random.split(key, 10)
        B, N, H = (8, 512, HIDDEN)
        s = 1.0 / np.sqrt(H)
        x = jax.random.normal(ks[0], (B, N, H), dtype=jnp.float32)
        adj = jax.random.randint(ks[1], (B, N, N), 0, 2, dtype=jnp.int32)
        Wq = jax.random.uniform(ks[2], (H, H), jnp.float32, -s, s)
        bq = jax.random.uniform(ks[3], (H,), jnp.float32, -s, s)
        Wk = jax.random.uniform(ks[4], (H, H), jnp.float32, -s, s)
        bk = jax.random.uniform(ks[5], (H,), jnp.float32, -s, s)
        Wv = jax.random.uniform(ks[6], (H, H), jnp.float32, -s, s)
        bv = jax.random.uniform(ks[7], (H,), jnp.float32, -s, s)
        gamma = jnp.ones((H,), jnp.float32)
        beta = jnp.zeros((H,), jnp.float32)
        return {'x': x, 'adj': adj, 'Wq': Wq, 'bq': bq, 'Wk': Wk, 'bk': bk, 'Wv': Wv, 'bv': bv, 'gamma': gamma, 'beta': beta}
    _L0_gnn_all = _L0_gnn_setup()
    _L0_gnn_in = {k: v for k, v in _L0_gnn_all.items() if k in ('Wq', 'bq', 'Wk', 'bk', 'Wv', 'bv', 'gamma', 'beta')}
    del _L0_gnn_all

    def _L1_gnn_setup():
        import jax, jax.numpy as jnp
        import numpy as np
        import math
        D = 256
        B, L = (8, 1024)
        EPS = 1e-05

        def layer_norm(y, gamma, beta):
            mu = jnp.mean(y, axis=-1, keepdims=True)
            var = jnp.mean(jnp.square(y - mu), axis=-1, keepdims=True)
            return (y - mu) * jax.lax.rsqrt(var + EPS) * gamma + beta
        key = jax.random.key(seed)
        ks = jax.random.split(key, 8)
        s = 1.0 / math.sqrt(D)
        x = jax.random.normal(ks[0], (B, L, D), dtype=jnp.float32)
        adj = jax.random.randint(ks[1], (B, L, L), 0, 2, dtype=jnp.int32)
        Wq = jax.random.normal(ks[2], (D, D), dtype=jnp.float32) * s
        Wk = jax.random.normal(ks[3], (D, D), dtype=jnp.float32) * s
        Wv = jax.random.normal(ks[4], (D, D), dtype=jnp.float32) * s
        Wo = jax.random.normal(ks[5], (D, D), dtype=jnp.float32) * s
        bo = jnp.zeros((D,), dtype=jnp.float32)
        gamma = jnp.ones((D,), dtype=jnp.float32)
        beta = jnp.zeros((D,), dtype=jnp.float32)
        return {'x': x, 'adj': adj, 'Wq': Wq, 'Wk': Wk, 'Wv': Wv, 'Wo': Wo, 'bo': bo, 'gamma': gamma, 'beta': beta}
    _L1_gnn_all = _L1_gnn_setup()
    _L1_gnn_in = {k: v for k, v in _L1_gnn_all.items() if k in ('Wq', 'Wk', 'Wv', 'Wo', 'bo', 'gamma', 'beta')}
    del _L1_gnn_all

    def _L2_gnn_setup():
        import jax, jax.numpy as jnp
        import numpy as np
        B, N, D, H = (4, 1024, 256, 8)
        HD = D // H
        EPS = 1e-05
        key = jax.random.key(seed)
        ks = jax.random.split(key, 12)
        x = jax.random.normal(ks[0], (B, N, D), dtype=jnp.float32)
        adj = jax.random.randint(ks[1], (B, N, N), 0, 2, dtype=jnp.int32)
        adj = jnp.maximum(adj, jnp.eye(N, dtype=jnp.int32)[None, :, :])
        s = 1.0 / np.sqrt(D)
        Wq = jax.random.uniform(ks[2], (D, D), jnp.float32, -s, s)
        bq = jnp.zeros((D,), jnp.float32)
        Wk = jax.random.uniform(ks[3], (D, D), jnp.float32, -s, s)
        bk = jnp.zeros((D,), jnp.float32)
        Wv = jax.random.uniform(ks[4], (D, D), jnp.float32, -s, s)
        bv = jnp.zeros((D,), jnp.float32)
        Wo = jax.random.uniform(ks[5], (D, D), jnp.float32, -s, s)
        bo = jnp.zeros((D,), jnp.float32)
        gamma = jnp.ones((D,), jnp.float32)
        beta = jnp.zeros((D,), jnp.float32)
        return {'x': x, 'adj': adj, 'Wq': Wq, 'bq': bq, 'Wk': Wk, 'bk': bk, 'Wv': Wv, 'bv': bv, 'Wo': Wo, 'bo': bo, 'gamma': gamma, 'beta': beta}
    _L2_gnn_all = _L2_gnn_setup()
    _L2_gnn_in = {k: v for k, v in _L2_gnn_all.items() if k in ('Wq', 'bq', 'Wk', 'bk', 'Wv', 'bv', 'Wo', 'bo', 'gamma', 'beta')}
    del _L2_gnn_all

    def _L3_gnn_setup():
        import jax, jax.numpy as jnp
        import numpy as np
        B, N, H, D = (8, 512, 256, 4)
        EPS = 1e-08
        LN_EPS = 1e-05

        def _linear(x, W, b):
            return x @ W.T + b
        key = jax.random.key(seed)
        ks = jax.random.split(key, 20)
        inp = {'adj': jax.random.randint(ks[0], (B, N, N), 0, D + 1, dtype=jnp.int32), 'relative_pos': jax.random.randint(ks[1], (B, N, N), 0, 16, dtype=jnp.int32), 'hid': jax.random.normal(ks[2], (B, N, H), dtype=jnp.float32), 'Wd': jax.random.normal(ks[3], (H, D * H), dtype=jnp.float32) * (1.0 / np.sqrt(D * H)), 'bd': jnp.zeros((H,), jnp.float32)}
        s = 1.0 / np.sqrt(H)
        for i, nm in enumerate(['ri', 'rh', 'zi', 'zh', 'ni', 'nh']):
            inp['W' + nm] = jax.random.normal(ks[4 + i], (H, H), dtype=jnp.float32) * s
            inp['b' + nm] = jnp.zeros((H,), jnp.float32)
        inp['gamma'] = jnp.ones((H,), jnp.float32)
        inp['beta'] = jnp.zeros((H,), jnp.float32)
        return inp
    _L3_gnn_all = _L3_gnn_setup()
    _L3_gnn_in = {k: v for k, v in _L3_gnn_all.items() if k in ('Wd', 'bd', 'Wri', 'bri', 'Wrh', 'brh', 'Wzi', 'bzi', 'Wzh', 'bzh', 'Wni', 'bni', 'Wnh', 'bnh', 'gamma', 'beta')}
    del _L3_gnn_all
    return {'x': x, 'adj': adj, 'L0_gnn_Wq': _L0_gnn_in['Wq'], 'L0_gnn_bq': _L0_gnn_in['bq'], 'L0_gnn_Wk': _L0_gnn_in['Wk'], 'L0_gnn_bk': _L0_gnn_in['bk'], 'L0_gnn_Wv': _L0_gnn_in['Wv'], 'L0_gnn_bv': _L0_gnn_in['bv'], 'L0_gnn_gamma': _L0_gnn_in['gamma'], 'L0_gnn_beta': _L0_gnn_in['beta'], 'L1_gnn_Wq': _L1_gnn_in['Wq'], 'L1_gnn_Wk': _L1_gnn_in['Wk'], 'L1_gnn_Wv': _L1_gnn_in['Wv'], 'L1_gnn_Wo': _L1_gnn_in['Wo'], 'L1_gnn_bo': _L1_gnn_in['bo'], 'L1_gnn_gamma': _L1_gnn_in['gamma'], 'L1_gnn_beta': _L1_gnn_in['beta'], 'L2_gnn_Wq': _L2_gnn_in['Wq'], 'L2_gnn_bq': _L2_gnn_in['bq'], 'L2_gnn_Wk': _L2_gnn_in['Wk'], 'L2_gnn_bk': _L2_gnn_in['bk'], 'L2_gnn_Wv': _L2_gnn_in['Wv'], 'L2_gnn_bv': _L2_gnn_in['bv'], 'L2_gnn_Wo': _L2_gnn_in['Wo'], 'L2_gnn_bo': _L2_gnn_in['bo'], 'L2_gnn_gamma': _L2_gnn_in['gamma'], 'L2_gnn_beta': _L2_gnn_in['beta'], 'L3_gnn_Wd': _L3_gnn_in['Wd'], 'L3_gnn_bd': _L3_gnn_in['bd'], 'L3_gnn_Wri': _L3_gnn_in['Wri'], 'L3_gnn_bri': _L3_gnn_in['bri'], 'L3_gnn_Wrh': _L3_gnn_in['Wrh'], 'L3_gnn_brh': _L3_gnn_in['brh'], 'L3_gnn_Wzi': _L3_gnn_in['Wzi'], 'L3_gnn_bzi': _L3_gnn_in['bzi'], 'L3_gnn_Wzh': _L3_gnn_in['Wzh'], 'L3_gnn_bzh': _L3_gnn_in['bzh'], 'L3_gnn_Wni': _L3_gnn_in['Wni'], 'L3_gnn_bni': _L3_gnn_in['bni'], 'L3_gnn_Wnh': _L3_gnn_in['Wnh'], 'L3_gnn_bnh': _L3_gnn_in['bnh'], 'L3_gnn_gamma': _L3_gnn_in['gamma'], 'L3_gnn_beta': _L3_gnn_in['beta']}

def reference(x, adj, L0_gnn_Wq, L0_gnn_bq, L0_gnn_Wk, L0_gnn_bk, L0_gnn_Wv, L0_gnn_bv, L0_gnn_gamma, L0_gnn_beta, L1_gnn_Wq, L1_gnn_Wk, L1_gnn_Wv, L1_gnn_Wo, L1_gnn_bo, L1_gnn_gamma, L1_gnn_beta, L2_gnn_Wq, L2_gnn_bq, L2_gnn_Wk, L2_gnn_bk, L2_gnn_Wv, L2_gnn_bv, L2_gnn_Wo, L2_gnn_bo, L2_gnn_gamma, L2_gnn_beta, L3_gnn_Wd, L3_gnn_bd, L3_gnn_Wri, L3_gnn_bri, L3_gnn_Wrh, L3_gnn_brh, L3_gnn_Wzi, L3_gnn_bzi, L3_gnn_Wzh, L3_gnn_bzh, L3_gnn_Wni, L3_gnn_bni, L3_gnn_Wnh, L3_gnn_bnh, L3_gnn_gamma, L3_gnn_beta):
    import jax
    import jax.numpy as jnp

    def _L0_gnn_ref(x, adj, Wq, bq, Wk, bk, Wv, bv, gamma, beta):
        import jax, jax.numpy as jnp
        import numpy as np
        HIDDEN = 256
        NHEADS = 8
        ALPHA = 0.1
        NUM_HOP = 4
        MASK_VAL = -16384.0
        LN_EPS = 1e-05
        B, N, H = x.shape
        u = H // NHEADS
        q = x @ Wq.T + bq
        k = x @ Wk.T + bk
        v = x @ Wv.T + bv
        qh = q.reshape(B, N, NHEADS, u).transpose(0, 2, 1, 3)
        kh = k.reshape(B, N, NHEADS, u).transpose(0, 2, 1, 3)
        vh = v.reshape(B, N, NHEADS, u).transpose(0, 2, 1, 3)
        scores = jnp.einsum('bhnd,bhmd->bhnm', qh, kh)
        mask = (adj == 0)[:, None, :, :]
        scores = jnp.where(mask, MASK_VAL, scores)
        pros = jax.nn.softmax(scores, axis=-1)
        z_init = vh
        z = z_init
        for _ in range(NUM_HOP):
            z = (1.0 - ALPHA) * jnp.einsum('bhnm,bhmd->bhnd', pros, z) + ALPHA * z_init
        h_prime = z.transpose(0, 2, 1, 3).reshape(B, N, H)
        y = x + h_prime
        mu = jnp.mean(y, axis=-1, keepdims=True)
        var = jnp.mean((y - mu) ** 2, axis=-1, keepdims=True)
        return (y - mu) / jnp.sqrt(var + LN_EPS) * gamma + beta

    def _L1_gnn_ref(x, adj, Wq, Wk, Wv, Wo, bo, gamma, beta):
        import jax, jax.numpy as jnp
        import numpy as np
        import math
        D = 256
        B, L = (8, 1024)
        EPS = 1e-05

        def layer_norm(y, gamma, beta):
            mu = jnp.mean(y, axis=-1, keepdims=True)
            var = jnp.mean(jnp.square(y - mu), axis=-1, keepdims=True)
            return (y - mu) * jax.lax.rsqrt(var + EPS) * gamma + beta
        d_out = Wq.shape[1]
        scale = 1.0 / math.sqrt(d_out)
        Q = x @ Wq
        K = x @ Wk
        V = x @ Wv
        sc = jnp.einsum('bld,bmd->blm', Q, K) * scale
        mask = adj == 0
        sc = jnp.where(mask, -jnp.inf, sc)
        all_inf = jnp.all(mask, axis=-1, keepdims=True)
        sc = jnp.where(all_inf, 0.0, sc)
        w = jax.nn.softmax(sc, axis=-1)
        out = jnp.einsum('blm,bmd->bld', w, V)
        y = x + out @ Wo + bo
        return layer_norm(y, gamma, beta)

    def _L2_gnn_ref(x, adj, Wq, bq, Wk, bk, Wv, bv, Wo, bo, gamma, beta):
        import jax, jax.numpy as jnp
        import numpy as np
        B, N, D, H = (4, 1024, 256, 8)
        HD = D // H
        EPS = 1e-05
        b, n, d = x.shape
        scale = 1.0 / np.sqrt(HD).astype(np.float32)
        q = (x @ Wq + bq).reshape(b, n, H, HD)
        k = (x @ Wk + bk).reshape(b, n, H, HD)
        v = (x @ Wv + bv).reshape(b, n, H, HD)
        scores = jnp.einsum('bnhd,bmhd->bhnm', q, k) * scale
        mask = (adj == 0)[:, None, :, :]
        scores = jnp.where(mask, jnp.float32(-jnp.inf), scores)
        attn = jax.nn.softmax(scores, axis=-1)
        h = jnp.einsum('bhnm,bmhd->bnhd', attn, v).reshape(b, n, d)
        h = h @ Wo + bo
        y = h + x
        mu = jnp.mean(y, axis=-1, keepdims=True)
        var = jnp.mean(jnp.square(y - mu), axis=-1, keepdims=True)
        return (y - mu) * jax.lax.rsqrt(var + EPS) * gamma + beta

    def _L3_gnn_ref(adj, relative_pos, hid, Wd, bd, Wri, bri, Wrh, brh, Wzi, bzi, Wzh, bzh, Wni, bni, Wnh, bnh, gamma, beta):
        import jax, jax.numpy as jnp
        import numpy as np
        B, N, H, D = (8, 512, 256, 4)
        EPS = 1e-08
        LN_EPS = 1e-05

        def _linear(x, W, b):
            return x @ W.T + b
        dt = hid.dtype
        labels = jnp.arange(1, D + 1, dtype=adj.dtype)
        mask = (adj[None] == labels[:, None, None, None]).astype(dt)
        weight = mask / (jnp.sum(mask, axis=-1, keepdims=True) + EPS)
        agg = jnp.einsum('dbmn,bnh->bmdh', weight, hid).reshape(hid.shape[0], hid.shape[1], D * H)
        out = jax.nn.relu(_linear(agg, Wd, bd))
        r = jax.nn.sigmoid(_linear(out, Wri, bri) + _linear(hid, Wrh, brh))
        z = jax.nn.sigmoid(_linear(out, Wzi, bzi) + _linear(hid, Wzh, bzh))
        n = jnp.tanh(_linear(out, Wni, bni) + r * _linear(hid, Wnh, bnh))
        out = (1.0 - z) * n + z * hid
        mu = jnp.mean(out, axis=-1, keepdims=True)
        var = jnp.var(out, axis=-1, keepdims=True)
        return (out - mu) / jnp.sqrt(var + LN_EPS) * gamma + beta
    x = _L0_gnn_ref(x, adj, L0_gnn_Wq, L0_gnn_bq, L0_gnn_Wk, L0_gnn_bk, L0_gnn_Wv, L0_gnn_bv, L0_gnn_gamma, L0_gnn_beta)
    x = _L1_gnn_ref(x, adj, L1_gnn_Wq, L1_gnn_Wk, L1_gnn_Wv, L1_gnn_Wo, L1_gnn_bo, L1_gnn_gamma, L1_gnn_beta)
    x = _L2_gnn_ref(x, adj, L2_gnn_Wq, L2_gnn_bq, L2_gnn_Wk, L2_gnn_bk, L2_gnn_Wv, L2_gnn_bv, L2_gnn_Wo, L2_gnn_bo, L2_gnn_gamma, L2_gnn_beta)
    x = _L3_gnn_ref(adj, adj, x, L3_gnn_Wd, L3_gnn_bd, L3_gnn_Wri, L3_gnn_bri, L3_gnn_Wrh, L3_gnn_brh, L3_gnn_Wzi, L3_gnn_bzi, L3_gnn_Wzh, L3_gnn_bzh, L3_gnn_Wni, L3_gnn_bni, L3_gnn_Wnh, L3_gnn_bnh, L3_gnn_gamma, L3_gnn_beta)
    return x

_drawn_inputs = setup_inputs


def setup_inputs(seed=0):
    import zlib

    import numpy as np

    out = dict(_drawn_inputs(seed))
    spreads = {'L0_gnn_gamma': (1.0, 0.2),
     'L0_gnn_beta': (0.0, 0.1),
     'L1_gnn_bo': (0.0, 0.1),
     'L1_gnn_gamma': (1.0, 0.2),
     'L1_gnn_beta': (0.0, 0.1),
     'L2_gnn_bq': (0.0, 0.8),
     'L2_gnn_bk': (0.0, 0.8),
     'L2_gnn_bv': (0.0, 0.1),
     'L2_gnn_bo': (0.0, 0.1),
     'L2_gnn_gamma': (1.0, 0.2),
     'L2_gnn_beta': (0.0, 0.1),
     'L3_gnn_bd': (0.0, 0.1),
     'L3_gnn_bri': (0.0, 0.657),
     'L3_gnn_brh': (0.0, 0.677),
     'L3_gnn_bzi': (0.0, 0.1),
     'L3_gnn_bzh': (0.0, 0.1),
     'L3_gnn_bni': (0.0, 0.1),
     'L3_gnn_bnh': (0.0, 0.1),
     'L3_gnn_gamma': (1.0, 0.2),
     'L3_gnn_beta': (0.0, 0.1)}
    factors = {'L0_gnn_bq': 5.099, 'L0_gnn_bk': 8.0, 'L3_gnn_Wri': 2.967}
    for name, (base, spread) in spreads.items():
        noise = np.random.default_rng([zlib.crc32(name.encode()), seed]).standard_normal(out[name].shape)
        drawn = base * np.exp(spread * noise) if base else spread * noise
        out[name] = jnp.asarray(drawn.astype(out[name].dtype))
    for name, factor in factors.items():
        out[name] = (out[name] * factor).astype(out[name].dtype)
    return out
```

```python
from contextlib import ExitStack

import numpy as np
import concourse.bass as bass
from concourse import mybir

P = 128
GRAPHS = 64
D = 256
NC = D // P
HEADS = 8
HD = D // HEADS
HC = P // HD
LABELS = 4
G = 2
UNITS = 2
ROUNDS = GRAPHS // (G * UNITS)
GN = G * P
LN_EPS = 1e-5
DEG_EPS = 1e-8
ALPHA = 0.1
HOPS = 4

ALU = mybir.AluOpType
ACT = mybir.ActivationFunctionType
AX_X = mybir.AxisListType.X
F32 = mybir.dt.float32
F32R = mybir.dt.float32r
I32 = mybir.dt.int32

SLOTS = ["q0", "k0", "v0", "q2", "k2", "v2", "d0", "d1", "d2", "d3",
         "ri", "zi", "ni", "rh", "zh", "nh"]
LOADED = len(SLOTS)
SLOT = {n: i for i, n in enumerate(SLOTS + ["g1", "vo1"])}
COLS = ["bq0", "bk0", "bv0", "bq2", "bk2", "bv2", "bd", "bri", "brh", "bzi", "bzh", "bni", "bnh",
        "gamma0", "beta0", "gamma1", "beta1", "gamma2", "beta2"]
COL = {n: NC * i for i, n in enumerate(COLS)}
ROWS = ["gamma0", "beta0", "gamma1", "beta1", "gamma2", "beta2", "gamma3", "beta3", "bo1", "bo2"]
ROW = {n: i for i, n in enumerate(ROWS)}


class Signal:

    def __init__(self, sems, per_round):
        self.sem, self.per_round = sems, per_round

    def __getitem__(self, u):
        return self.sem[u]

    def at(self, it, k):
        return it * self.per_round + k


class Own:

    def __init__(self, sem, per_round):
        self.sem, self.per_round, self.used = sem, per_round, 0

    def next(self, it):
        self.used += 1
        return it * self.per_round + self.used


DVE_OWN = 190
POOL_OWN = 8


def gnn_program(nc, x, xt, adj, weights, l1_weights, wo2, cols, rows, out):
    ctx = ExitStack()
    with ctx:
        def sb(name, shape, dt=F32):
            return ctx.enter_context(nc.sbuf_tensor(name, shape, dt))

        def sem(name):
            return ctx.enter_context(nc.semaphore(name))

        def per_unit(name, shape, dt=F32):
            return [sb(f"{name}_{u}", shape, dt) for u in range(UNITS)]

        def aliased(name, over, shape, dt):
            return [nc.alloc_sbuf_tensor_at(f"{name}_{u}", shape, dt, offset=nc.lookup_mloc(over[u]).addr) for u in range(UNITS)]

        ident = sb("ident", [P, P])
        w_hi = sb("w_hi", [P, len(SLOT), NC, D], F32R)
        w_lo = sb("w_lo", [P, len(SLOT), NC, D], F32R)
        wo2_sb = sb("wo2_sb", [P, NC, D])
        col = sb("col", [P, NC * len(COLS)])
        half = sb("half", [P, 2 * NC])
        row = sb("row", [P, len(ROWS), D])
        fill = sb("fill", [P, 3])
        magic = sb("magic", [P, G], I32)
        pidle = sb("pidle", [P, 1])
        psink = [sb(f"psink_{u}", [P, 1]) for u in range(2)]

        x_in = per_unit("x_in", [P, G, D])
        xt_in = per_unit("xt_in", [P, NC, G, P])
        adj_in = per_unit("adj_in", [P, G, P], I32)
        absent = per_unit("absent", [P, G, P], I32)
        adj_f = per_unit("adj_f", [P, G, P])
        xT = per_unit("xT", [P, NC, GN])
        xT_hi = per_unit("xT_hi", [P, NC, GN], F32R)
        xT_lo = per_unit("xT_lo", [P, NC, GN], F32R)
        xnat = per_unit("xnat", [P, G, D])
        y = per_unit("y", [P, G, D])
        qT = per_unit("qT", [P, NC, GN])
        kT = per_unit("kT", [P, NC, GN])
        vT = per_unit("vT", [P, NC, GN])
        vnat = per_unit("vnat", [P, G, D])
        kblk = per_unit("kblk", [P, NC, G, HC, P])
        E = per_unit("E", [P, G, NC, HC, P])
        PT = per_unit("PT", [P, G, NC, HC, P])
        wT = per_unit("wT", [P, G, LABELS, P])
        oT_hi = per_unit("oT_hi", [P, NC, GN], F32R)
        oT_lo = per_unit("oT_lo", [P, NC, GN], F32R)
        nmax = per_unit("nmax", [P, G, NC, HC])
        rmax = per_unit("rmax", [P, G, NC, HC])
        esum = per_unit("esum", [P, G, NC, HC])
        rsum = per_unit("rsum", [P, G, NC, HC])
        cnt = per_unit("cnt", [P, G, LABELS])
        rcnt = per_unit("rcnt", [P, G, LABELS])
        stats = per_unit("stats", [P, G, 6])
        mv = per_unit("mv", [P, G, 2])
        var = per_unit("var", [P, G])
        rstd = per_unit("rstd", [P, G])
        seed = per_unit("seed", [P, G], I32)
        nt = per_unit("nt", [P, G])
        zT, rT = kT, kT
        agg_hi = aliased("agg_hi", E, [P, NC, LABELS, G, P], F32R)
        agg_lo = aliased("agg_lo", PT, [P, NC, LABELS, G, P], F32R)

        ps = [[ctx.enter_context(nc.psum_tensor(f"bank_{u}_{b}", [P, 512], F32)) for b in range(4)]
              for u in range(UNITS)]

        def signal(name, per_round):
            return Signal([sem(f"{name}_{u}") for u in range(UNITS)], per_round)

        loaded = signal("loaded", 4 * 16)
        adj_ready = signal("adj_ready", 1)
        x0_hi = signal("x0_hi", 1)
        xt32 = signal("xt32", 3)
        xt_ready = signal("xt_ready", 4)
        proj = signal("proj", 8)
        q_ready = signal("q_ready", 3)
        k_ready = signal("k_ready", 2)
        kblk_ready = signal("kblk_ready", 2)
        v_ready = signal("v_ready", 2)
        vback = signal("vback", 2)
        vn_ready = signal("vn_ready", 3)
        s_ready = signal("s_ready", 9)
        max_ready = signal("max_ready", 9)
        exp_ready = signal("exp_ready", 9)
        r_ready = signal("r_ready", 9)
        e_ready = signal("e_ready", 9)
        p_t = signal("p_t", 9)
        pt_ready = signal("pt_ready", 9)
        o_t = signal("o_t", 10)
        zt_ready = signal("zt_ready", 10)
        back = signal("back", 11)
        z_ready = signal("z_ready", 6)
        nrm_ready = signal("nrm_ready", 4)
        n_t = signal("n_t", 3)
        xn_ready = signal("xn_ready", 4)
        wm_cnt = signal("wm_cnt", 1)
        wm_ready = signal("wm_ready", 1)
        w_t = signal("w_t", 2)
        wt_ready = signal("wt_ready", 2)
        agg = signal("agg", 4)
        agg_hi_ready = signal("agg_hi_ready", 4)
        agg_lo_ready = signal("agg_lo_ready", 4)
        out_t = signal("out_t", 1)
        out32 = signal("out32", 1)
        out_ready = signal("out_ready", 1)
        gates = signal("gates", 3)
        gate_ready = signal("gate_ready", 3)
        r_used = signal("r_used", 1)
        mixed = signal("mixed", 1)
        mixed_t = signal("mixed_t", 1)
        stored = signal("stored", 16)

        w_loaded = [sem(f"w_loaded_{j}") for j in range(LOADED // 4 + 1)]
        c_loaded, w_split, w_read, l1_prod, consts = (
            sem(n) for n in ("c_loaded", "w_split", "w_read", "l1_prod", "consts"))
        wmade = sem("wmade")
        dve_own, pool_own = Own(sem("dve_own"), DVE_OWN), Own(sem("pool_own"), POOL_OWN)
        dve_pre, pool_pre = sem("dve_pre"), sem("pool_pre")

        UR = range(UNITS)
        ORDER = [(step, u) for step in
                 ["in", "qkv0", "soft0", "hop0", "hop1", "hop2", "hop3", "norm1", "l1a", "l1b", "norm2",
                  "qkv2", "soft2", "pv2", "norm3", "agg", "out", "gate", "fin"] for u in UR]

        x_v = x.rearrange("(r u g) n d -> r u n g d", u=UNITS, g=G)
        xt_v = xt.rearrange("(r u g) (c p) n -> r u p c g n", u=UNITS, g=G, p=P)
        adj_v = adj.rearrange("(r u g) n m -> r u n g m", u=UNITS, g=G)
        out_v = out.rearrange("(r u g) n d -> r u n g d", u=UNITS, g=G)

        def rowc(name, n=G):
            return row[:, ROW[name]:ROW[name] + 1, :].to_broadcast([P, n, D])

        def colc(name, c):
            return col[:, COL[name] + c:COL[name] + c + 1]

        def flat(t):
            return t[:].rearrange("p a b -> p (a b)")

        stage = [kblk[j][:].rearrange("p c g h n -> p (c g h n)").rearrange("p (s c d) -> p s c d", s=4, c=NC)
                 for j in UR]
        WR = LOADED // 4
        block = ctx.enter_context(nc.Block())

        @block.sync
        def _(sp):
            sp.dma_start(col[:], cols).then_inc(c_loaded, 16)
            sp.dma_start(row[:], rows.unsqueeze(0).to_broadcast([P, len(ROWS), D])).then_inc(c_loaded, 16)
            sp.dma_start(wo2_sb[:], wo2).then_inc(c_loaded, 16)
            for j in range(WR):
                if j >= 2:
                    sp.wait_ge(w_split, j - 1)
                sp.dma_start(stage[j % 2], weights[:, 4 * j:4 * j + 4]).then_inc(w_loaded[j], 16)
            sp.wait_ge(w_split, WR - 1)
            sp.dma_start(stage[WR % 2], l1_weights).then_inc(w_loaded[WR], 16)

            def load(r, u):
                sp.dma_start(x_in[u][:], x_v[r, u]).then_inc(loaded[u], 16)
                for c in range(NC):
                    sp.dma_start(xt_in[u][:, c], xt_v[r, u][:, c]).then_inc(loaded[u], 16)
                sp.dma_start(adj_in[u][:], adj_v[r, u]).then_inc(loaded[u], 16)

            def store(r, u, it):
                sp.wait_ge(xn_ready[u], xn_ready.at(it, 4))
                sp.dma_start(out_v[r, u], xnat[u][:]).then_inc(stored[u], 16)

            for u in UR:
                load(0, u)
            with sp.Fori(0, ROUNDS - 1) as it:
                for u in UR:
                    sp.wait_ge(adj_ready[u], adj_ready.at(it, 1))
                    sp.wait_ge(nrm_ready[u], nrm_ready.at(it, 1))
                    load(it + 1, u)
                for u in UR:
                    store(it, u, it)
            for u in UR:
                store(ROUNDS - 1, u, ROUNDS - 1)
                sp.wait_ge(stored[u], stored.at(ROUNDS, 16))

        @block.tensor
        def _(pe):
            def split_product(o, w, n, xh, xl, first, last, count=1):
                for kc in range(NC):
                    for j, (a, b) in enumerate(((w_hi, xh), (w_hi, xl), (w_lo, xh))):
                        mm = nc.tensor.matmul(o[0], a[:, n, kc, o[1] * P:(o[1] + 1) * P], b(kc),
                                              start=first and kc == 0 and j == 0,
                                              stop=last and kc == NC - 1 and j == 2)
                return mm

            def project(bank, names, u):
                for oc in range(NC):
                    for i, (n, hi, lo) in enumerate(names):
                        mm = split_product((bank[:, oc * GN:(oc + 1) * GN], oc), None, SLOT[n], hi, lo,
                                           i == 0, i == len(names) - 1)
                return mm

            pe.wait_ge(w_loaded[WR], 16)
            s = stage[WR % 2]
            for b, (i, j) in enumerate(((0, 1), (2, 3))):
                for kc in range(NC):
                    for jc in range(NC):
                        mm = nc.tensor.matmul(ps[0][b][:, kc * D:(kc + 1) * D], s[:, i, jc, kc * P:(kc + 1) * P],
                                              s[:, j, jc, :], start=jc == 0, stop=jc == NC - 1)
                mm.then_inc(l1_prod, 1)
            pe.wait_ge(wmade, 1)

            with pe.Fori(0, ROUNDS) as it:
                def x_parts(u):
                    return (lambda kc: xT_hi[u][:, kc, :], lambda kc: xT_lo[u][:, kc, :])

                for step, u in ORDER:
                    b = ps[u]
                    if step in ("qkv0", "qkv2"):
                        L = int(step[-1])
                        a = 0 if L == 0 else 1
                        pe.wait_ge(xt_ready[u], xt_ready.at(it, L + 1))
                        for i, n in enumerate("qkv"):
                            project(b[i], [(f"{n}{L}", *x_parts(u))], u).then_inc(proj[u], 1)
                        pe.wait_ge(v_ready[u], v_ready.at(it, a + 1))
                        for g in range(G):
                            for c in range(NC):
                                mm = nc.tensor.transpose(b[3][:, (g * NC + c) * P:(g * NC + c + 1) * P],
                                                         vT[u][:, c, g * P:(g + 1) * P], ident[:])
                        mm.then_inc(vback[u], 1)
                        pe.wait_ge(q_ready[u], q_ready.at(it, L + 1))
                        pe.wait_ge(kblk_ready[u], kblk_ready.at(it, a + 1))
                        for g in range(G):
                            for c in range(NC):
                                if (g, c) == (1, 1):
                                    pe.wait_ge(vn_ready[u], vn_ready.at(it, L + 1))
                                nc.tensor.matmul(b[g * NC + c][:, :], qT[u][:, c, g * P:(g + 1) * P],
                                                 kblk[u][:, c, g].rearrange("p h n -> p (h n)"),
                                                 start=True, stop=True).then_inc(s_ready[u], 1)
                    if step in ("soft0", "soft2"):
                        k0 = 0 if step == "soft0" else 5
                        for g in range(G):
                            for c in range(NC):
                                k = g * NC + c
                                pe.wait_ge(e_ready[u], e_ready.at(it, k0 + k + 1))
                                for h in range(HC):
                                    mm = nc.tensor.transpose(b[k][:, h * P:(h + 1) * P], E[u][:, g, c, h], ident[:])
                                mm.then_inc(p_t[u], 1)
                    if step[:3] == "hop" or step == "pv2":
                        t = int(step[3]) if step[0] == "h" else HOPS
                        if t == 0:
                            pe.wait_ge(pt_ready[u], pt_ready.at(it, 4))
                        if t == HOPS:
                            pe.wait_ge(pt_ready[u], pt_ready.at(it, 9))
                        for g in range(G):
                            if 0 < t < HOPS:
                                pe.wait_ge(z_ready[u], z_ready.at(it, G * (t - 1) + g + 1))
                            for h in range(HEADS):
                                c, hh = divmod(h, HC)
                                mm = nc.tensor.matmul(b[g][hh * HD:(hh + 1) * HD, c * P:(c + 1) * P],
                                                      vnat[u][:, g, h * HD:(h + 1) * HD], PT[u][:, g, c, hh],
                                                      start=True, stop=True)
                            mm.then_inc(o_t[u], 1)
                        for g in range(G):
                            pe.wait_ge(zt_ready[u], zt_ready.at(it, G * t + g + 1))
                            for c in range(NC):
                                zc = zT[u][:, c, g * P:(g + 1) * P]
                                if t < HOPS:
                                    mm = nc.tensor.transpose(b[2 + g][:, c * P:(c + 1) * P], zc, ident[:])
                                else:
                                    mm = nc.tensor.matmul(b[2 + g][:, 0:D], zc, wo2_sb[:, c, :],
                                                          start=c == 0, stop=c == NC - 1)
                            mm.then_inc(back[u], 1)
                    if step[:4] == "norm":
                        L = int(step[-1])
                        pe.wait_ge(nrm_ready[u], nrm_ready.at(it, L))
                        for c in range(NC):
                            for g in range(G):
                                mm = nc.tensor.transpose(b[0][:, c * GN + g * P:c * GN + (g + 1) * P],
                                                         y[u][:, g, c * P:(c + 1) * P], ident[:])
                        mm.then_inc(n_t[u], 1)
                    if step == "l1a":
                        pe.wait_ge(xt_ready[u], xt_ready.at(it, 2))
                        project(b[0], [("g1", *x_parts(u))], u).then_inc(proj[u], 1)
                        n = SLOT["vo1"]
                        for g in range(G):
                            for c in range(NC):
                                xs = slice(g * P, (g + 1) * P)
                                for j, (a, w) in enumerate(((xT_hi, w_hi), (xT_lo, w_hi), (xT_hi, w_lo))):
                                    mm = nc.tensor.matmul(b[1][:, g * D:(g + 1) * D], a[u][:, c, xs], w[:, n, c, :],
                                                          start=c == 0 and j == 0, stop=c == NC - 1 and j == 2)
                        mm.then_inc(proj[u], 1)
                        pe.wait_ge(q_ready[u], q_ready.at(it, 2))
                        for g in range(G):
                            for c in range(NC):
                                xs = slice(g * P, (g + 1) * P)
                                mm = nc.tensor.matmul(b[2][:, g * P:(g + 1) * P], qT[u][:, c, xs], xT[u][:, c, xs],
                                                      start=c == 0, stop=c == NC - 1)
                        mm.then_inc(s_ready[u], 1)
                    if step == "l1b":
                        pe.wait_ge(e_ready[u], e_ready.at(it, 5))
                        for g in range(G):
                            mm = nc.tensor.transpose(b[3][:, g * P:(g + 1) * P], E[u][:, g, 0, 0], ident[:])
                        mm.then_inc(p_t[u], 1)
                        pe.wait_ge(pt_ready[u], pt_ready.at(it, 5))
                        pe.wait_ge(vn_ready[u], vn_ready.at(it, 2))
                        for g in range(G):
                            mm = nc.tensor.matmul(b[0][:, g * D:(g + 1) * D], PT[u][:, g, 0, 0], vnat[u][:, g, :],
                                                  start=True, stop=True)
                        mm.then_inc(back[u], 1)
                    if step == "agg":
                        pe.wait_ge(wm_ready[u], wm_ready.at(it, 1))
                        pe.wait_ge(xt_ready[u], xt_ready.at(it, 4))
                        for g in range(G):
                            for d in range(LABELS):
                                mm = nc.tensor.transpose(b[g][:, d * P:(d + 1) * P], E[u][:, g, 0, d], ident[:])
                            mm.then_inc(w_t[u], 1)
                        pe.wait_ge(xn_ready[u], xn_ready.at(it, 3))
                        pe.wait_ge(wt_ready[u], wt_ready.at(it, 2))
                        for g in range(G):
                            for c in range(NC):
                                nc.tensor.matmul(b[g * NC + c][:, :], xnat[u][:, g, c * P:(c + 1) * P],
                                                 wT[u][:, g].rearrange("p d n -> p (d n)"),
                                                 start=True, stop=True).then_inc(agg[u], 1)
                    if step == "out":
                        pe.wait_ge(agg_lo_ready[u], agg_lo_ready.at(it, 4))
                        project(b[0], [(f"d{d}",
                                        (lambda kc, d=d: agg_hi[u][:, kc, d].rearrange("p g n -> p (g n)")),
                                        (lambda kc, d=d: agg_lo[u][:, kc, d].rearrange("p g n -> p (g n)")))
                                       for d in range(LABELS)], u).then_inc(out_t[u], 1)
                        project(b[3], [("nh", *x_parts(u))], u)
                    if step == "gate":
                        o_parts = (lambda kc: oT_hi[u][:, kc, :], lambda kc: oT_lo[u][:, kc, :])
                        pe.wait_ge(out_ready[u], out_ready.at(it, 1))
                        project(b[1], [("rh", *x_parts(u)), ("ri", *o_parts)], u).then_inc(gates[u], 1)
                        project(b[2], [("zh", *x_parts(u)), ("zi", *o_parts)], u).then_inc(gates[u], 1)
                        project(b[0], [("ni", *o_parts)], u).then_inc(gates[u], 1)
                    if step == "fin":
                        pe.wait_ge(mixed[u], mixed.at(it, 1))
                        for g in range(G):
                            for c in range(NC):
                                mm = nc.tensor.transpose(b[1][:, g * D + c * P:g * D + (c + 1) * P],
                                                         qT[u][:, c, g * P:(g + 1) * P], ident[:])
                        mm.then_inc(mixed_t[u], 1)

        @block.scalar
        def _(act):
            for j in range(WR):
                act.wait_ge(w_loaded[j], 16)
                nc.scalar.activation(w_hi[:, 4 * j:4 * j + 4].rearrange("p s c d -> p (s c d)"),
                                     stage[j % 2].rearrange("p s c d -> p (s c d)"), ACT.Copy).then_inc(w_read, 1)
            for b, (n, scale) in enumerate((("g1", float(D) ** -0.5), ("vo1", 1.0))):
                act.wait_ge(l1_prod, b + 1)
                nc.scalar.activation(w_hi[:, SLOT[n]].rearrange("p c d -> p (c d)"), ps[0][b][:, :], ACT.Copy,
                                     scale=scale).then_inc(w_read, 1)
            act.wait_ge(wmade, 1)
            with act.Fori(0, ROUNDS) as it:
                for step, u in ORDER:
                    b = ps[u]
                    if step == "in":
                        act.wait_ge(loaded[u], loaded.at(it, 64))
                        nc.scalar.activation(adj_f[u][:], adj_in[u][:], ACT.Copy)
                        nc.scalar.activation(flat(xT_hi[u]), xt_in[u][:].rearrange("p c g n -> p (c g n)"),
                                             ACT.Copy).then_inc(x0_hi[u], 1)
                    if step in ("qkv0", "qkv2"):
                        L = int(step[-1])
                        p0 = 0 if L == 0 else 5
                        for i, (n, t, ready, k) in enumerate((("q", qT, q_ready, L + 1),
                                                             ("k", kT, k_ready, L // 2 + 1),
                                                             ("v", vT, v_ready, L // 2 + 1))):
                            act.wait_ge(proj[u], proj.at(it, p0 + i + 1))
                            for c in range(NC):
                                a = nc.scalar.activation(t[u][:, c, :], b[i][:, c * GN:(c + 1) * GN], ACT.Identity,
                                                         bias=colc(f"b{n}{L}", c))
                            a.then_inc(ready[u], 1)
                        act.wait_ge(vback[u], vback.at(it, L // 2 + 1))
                        nc.scalar.activation(flat(vnat[u]), b[3][:, :], ACT.Copy).then_inc(vn_ready[u], 1)
                    if step in ("soft0", "soft2"):
                        k0 = 0 if step == "soft0" else 5
                        scale = 1.0 if step == "soft0" else float(HD) ** -0.5
                        for k in range(G * NC):
                            g, c = divmod(k, NC)
                            act.wait_ge(max_ready[u], max_ready.at(it, k0 + k + 1))
                            for h in range(HC):
                                a = nc.scalar.activation(E[u][:, g, c, h], b[k][:, h * P:(h + 1) * P], ACT.Exp,
                                                         bias=nmax[u][:, g, c, h:h + 1], scale=scale,
                                                         accum_out=esum[u][:, g, c, h:h + 1])
                            a.then_inc(exp_ready[u], 1)
                        for k in range(G * NC):
                            g, c = divmod(k, NC)
                            act.wait_ge(p_t[u], p_t.at(it, k0 + k + 1))
                            nc.scalar.activation(PT[u][:, g, c].rearrange("p h n -> p (h n)"), b[k][:, :],
                                                 ACT.Copy).then_inc(pt_ready[u], 1)
                    if step[:3] == "hop" and step != "hop3":
                        t = int(step[3])
                        for g in range(G):
                            act.wait_ge(back[u], back.at(it, G * t + g + 1))
                            nc.scalar.activation(vnat[u][:, g, :], b[2 + g][:, 0:D], ACT.Copy).then_inc(z_ready[u], 1)
                    if step[:4] == "norm":
                        L = int(step[-1])
                        act.wait_ge(n_t[u], n_t.at(it, L))
                        for c in range(NC):
                            a = nc.scalar.activation(xT[u][:, c, :], b[0][:, c * GN:(c + 1) * GN], ACT.Identity,
                                                     bias=colc(f"beta{L - 1}", c), scale=colc(f"gamma{L - 1}", c))
                        a.then_inc(xt32[u], 1)
                    if step == "l1a":
                        act.wait_ge(proj[u], proj.at(it, 4))
                        nc.scalar.activation(flat(qT[u]), b[0][:, :], ACT.Copy).then_inc(q_ready[u], 1)
                        act.wait_ge(proj[u], proj.at(it, 5))
                        nc.scalar.activation(flat(vnat[u]), b[1][:, :], ACT.Copy).then_inc(vn_ready[u], 1)
                    if step == "l1b":
                        act.wait_ge(max_ready[u], max_ready.at(it, 5))
                        for g in range(G):
                            a = nc.scalar.activation(E[u][:, g, 0, 0], b[2][:, g * P:(g + 1) * P], ACT.Exp,
                                                     bias=nmax[u][:, g, 0, 0:1], accum_out=esum[u][:, g, 0, 0:1])
                        a.then_inc(exp_ready[u], 1)
                        act.wait_ge(p_t[u], p_t.at(it, 5))
                        nc.scalar.activation(PT[u][:, :, 0, 0], b[3][:, 0:GN].rearrange("p (g n) -> p g n", g=G),
                                             ACT.Copy).then_inc(pt_ready[u], 1)
                    if step == "agg":
                        for g in range(G):
                            act.wait_ge(w_t[u], w_t.at(it, g + 1))
                            nc.scalar.activation(wT[u][:, g].rearrange("p d n -> p (d n)"), b[g][:, :],
                                                 ACT.Copy).then_inc(wt_ready[u], 1)
                        for k in range(G * NC):
                            g, c = divmod(k, NC)
                            act.wait_ge(agg[u], agg.at(it, k + 1))
                            nc.scalar.activation(agg_hi[u][:, c, :, g, :],
                                                 b[k][:, :].rearrange("p (d n) -> p d n", d=LABELS),
                                                 ACT.Copy).then_inc(agg_hi_ready[u], 1)
                    if step == "out":
                        act.wait_ge(out_t[u], out_t.at(it, 1))
                        for c in range(NC):
                            a = nc.scalar.activation(qT[u][:, c, :], b[0][:, c * GN:(c + 1) * GN], ACT.Relu,
                                                     bias=colc("bd", c))
                        a.then_inc(out32[u], 1)
                    if step == "gate":
                        for i, t in enumerate((rT, vT)):
                            act.wait_ge(gates[u], gates.at(it, i + 1))
                            for c in range(NC):
                                a = nc.scalar.activation(t[u][:, c, :], b[i + 1][:, c * GN:(c + 1) * GN], ACT.Tanh,
                                                         bias=half[:, NC * i + c:NC * i + c + 1], scale=0.5)
                            a.then_inc(gate_ready[u], 1)
                        act.wait_ge(r_used[u], r_used.at(it, 1))
                        for c in range(NC):
                            v = vnat[u][:, c, :]
                            a = nc.scalar.activation(v, v, ACT.Tanh, bias=colc("bni", c))
                        a.then_inc(gate_ready[u], 1)

        @block.gpsimd
        def _(pool):
            own = pool_own

            nc.gpsimd.memset(pidle[:], 0.0)
            nc.gpsimd.memset(ident[:], 0.0).then_inc(pool_pre, 1)
            pool.wait_ge(pool_pre, 1)
            nc.gpsimd.affine_select(out=ident[:], in_=ident[:], compare_op=ALU.not_equal, fill=1.0, base=0,
                                    pattern=[[-1, P]], channel_multiplier=1).then_inc(consts, 1)
            for u in UR:
                pool.sem_inc(stored[u], 16)
            pool.wait_ge(wmade, 1)
            with pool.Fori(0, ROUNDS) as it:
                def scale_shift(u, gamma, beta):
                    nc.gpsimd.tensor_tensor(xnat[u][:], y[u][:], rowc(gamma), ALU.mult).then_inc(own.sem, 1)
                    pool.wait_ge(own.sem, own.next(it))
                    return nc.gpsimd.tensor_tensor(xnat[u][:], xnat[u][:], rowc(beta), ALU.add)

                for step, u in ORDER:
                    if step == "in":
                        pool.wait_ge(loaded[u], loaded.at(it, 64))
                        nc.gpsimd.tensor_tensor(psink[u][:], pidle[:], pidle[:], ALU.mult)
                        nc.gpsimd.tensor_scalar(absent[u][:], adj_in[u][:], 0.0, None, ALU.is_equal)\
                            .then_inc(adj_ready[u], 1)
                    if step in ("soft0", "soft2", "l1b"):
                        k0 = {"soft0": 0, "l1b": 4, "soft2": 5}[step]
                        for k in range(1 if step == "l1b" else G * NC):
                            g, c = divmod(k, NC)
                            pool.wait_ge(r_ready[u], r_ready.at(it, k0 + k + 1))
                            if step == "l1b":
                                e, r = E[u][:, :, 0, 0], rsum[u][:, :, 0, 0:1].to_broadcast([P, G, P])
                            else:
                                e, r = E[u][:, g, c], rsum[u][:, g, c].unsqueeze(2).to_broadcast([P, HC, P])
                            nc.gpsimd.tensor_tensor(e, e, r, ALU.mult).then_inc(e_ready[u], 1)
                    if step[:4] == "norm":
                        L = int(step[-1])
                        pool.wait_ge(nrm_ready[u], nrm_ready.at(it, L))
                        if L == 1:
                            pool.wait_ge(stored[u], stored.at(it, 16))
                        scale_shift(u, f"gamma{L - 1}", f"beta{L - 1}").then_inc(xn_ready[u], 1)
                    if step == "agg":
                        pool.wait_ge(wm_cnt[u], wm_cnt.at(it, 1))
                        for g in range(G):
                            w = E[u][:, g, 0]
                            a = nc.gpsimd.tensor_tensor(w, w, rcnt[u][:, g].unsqueeze(2).to_broadcast([P, LABELS, P]),
                                                        ALU.mult)
                        a.then_inc(wm_ready[u], 1)
                    if step == "fin":
                        pool.wait_ge(nrm_ready[u], nrm_ready.at(it, 4))
                        scale_shift(u, "gamma3", "beta3").then_inc(xn_ready[u], 1)
                used = own.used
            assert used == POOL_OWN, used

        @block.vector
        def _(dve):
            own = dve_own
            pre = [0]

            def settle(ins):
                pre[0] += 1
                ins.then_inc(dve_pre, 1)
                dve.wait_ge(dve_pre, pre[0])

            for L, v in enumerate((-16384.0, -1e30, -3e38)):
                nc.vector.memset(fill[:, L:L + 1], v)
            dve.wait_ge(c_loaded, 48)
            for i, n in enumerate("rz"):
                for c in range(NC):
                    settle(nc.vector.tensor_tensor(half[:, NC * i + c:NC * i + c + 1], colc(f"b{n}i", c),
                                                   colc(f"b{n}h", c), ALU.add))
            settle(nc.vector.tensor_scalar(half[:], half[:], 0.5, None, ALU.mult))
            for j in range(WR):
                dve.wait_ge(w_read, j + 1)
                nc.vector.tensor_tensor(w_lo[:, 4 * j:4 * j + 4].rearrange("p s c d -> p (s c d)"),
                                        stage[j % 2].rearrange("p s c d -> p (s c d)"),
                                        w_hi[:, 4 * j:4 * j + 4].bitcast(F32).rearrange("p s c d -> p (s c d)"),
                                        ALU.subtract).then_inc(w_split, 1)
            for b, (n, scale) in enumerate((("g1", float(D) ** -0.5), ("vo1", 1.0))):
                dve.wait_ge(w_read, WR + b + 1)
                settle(nc.vector.scalar_tensor_tensor(w_lo[:, SLOT[n]].rearrange("p c d -> p (c d)"), ps[0][b][:, :],
                                                      scale, w_hi[:, SLOT[n]].bitcast(F32).rearrange("p c d -> p (c d)"),
                                                      ALU.mult, ALU.subtract))
            dve.wait_ge(consts, 1)
            for u in UR:
                settle(nc.vector.memset(kblk[u][:], 0.0))
            nc.vector.memset(magic[:], 0x5F3759DF).then_inc(wmade, 1)

            with dve.Fori(0, ROUNDS) as it:
                def link(ins):
                    ins.then_inc(own.sem, 1)
                    dve.wait_ge(own.sem, own.next(it))

                def layer_norm(u, src):
                    for g in range(G):
                        a = nc.vector.bn_stats(stats[u][:, g, :], src[g])
                    link(a)
                    nc.vector.memset(var[u][:], 0.0)
                    for g in range(G):
                        a = nc.vector.bn_aggr(mv[u][:, g, :], stats[u][:, g, :])
                    link(a)
                    link(nc.vector.tensor_scalar(var[u][:], mv[u][:, :, 1], LN_EPS, None, ALU.add))
                    link(nc.vector.tensor_scalar(seed[u][:], var[u][:].bitcast(I32), 1, None,
                                                 ALU.arith_shift_right))
                    link(nc.vector.tensor_tensor(rstd[u][:].bitcast(I32), magic[:], seed[u][:], ALU.subtract))
                    for _ in range(3):
                        link(nc.vector.scalar_tensor_tensor(nt[u][:], rstd[u][:], -0.5, rstd[u][:], ALU.mult, ALU.mult))
                        link(nc.vector.tensor_tensor(nt[u][:], nt[u][:], var[u][:], ALU.mult))
                        link(nc.vector.scalar_tensor_tensor(rstd[u][:], nt[u][:], 1.5, rstd[u][:], ALU.add, ALU.mult))
                    for g in range(G):
                        a = nc.vector.tensor_scalar(y[u][:, g, :], src[g], mv[u][:, g, 0:1], rstd[u][:, g:g + 1],
                                                    ALU.subtract, ALU.mult)
                    a.then_inc(nrm_ready[u], 1)

                for step, u in ORDER:
                    b = ps[u]
                    if step == "in":
                        dve.wait_ge(x0_hi[u], x0_hi.at(it, 1))
                        nc.vector.tensor_tensor(flat(xT_lo[u]), xt_in[u][:].rearrange("p c g n -> p (c g n)"),
                                                flat(xT_hi[u]).bitcast(F32), ALU.subtract).then_inc(xt_ready[u], 1)
                    if step in ("qkv0", "qkv2"):
                        a = int(step[-1]) // 2
                        dve.wait_ge(k_ready[u], k_ready.at(it, a + 1))
                        for h in range(HC):
                            q = slice(h * HD, (h + 1) * HD)
                            cp = nc.vector.tensor_copy(kblk[u][q, :, :, h, :],
                                                       kT[u][q].rearrange("p c (g n) -> p c g n", g=G))
                        cp.then_inc(kblk_ready[u], 1)
                    if step in ("soft0", "soft2", "l1b"):
                        k0 = {"soft0": 0, "l1b": 4, "soft2": 5}[step]
                        L = {"soft0": 0, "l1b": 1, "soft2": 2}[step]
                        scale = {"soft0": 1.0, "l1b": 1.0, "soft2": float(HD) ** -0.5}[step]
                        if step == "soft0":
                            dve.wait_ge(adj_ready[u], adj_ready.at(it, 1))
                        ks = range(1 if step == "l1b" else G * NC)

                        def views(k):
                            g, c = divmod(k, NC)
                            if step == "l1b":
                                return (b[2][:, 0:GN].rearrange("p (g n) -> p g n", g=G), absent[u][:],
                                        rmax[u][:, :, 0, 0], nmax[u][:, :, 0, 0], esum[u][:, :, 0, 0],
                                        rsum[u][:, :, 0, 0], G)
                            return (b[k][:, :].rearrange("p (h n) -> p h n", h=HC),
                                    absent[u][:, g:g + 1, :].to_broadcast([P, HC, P]),
                                    rmax[u][:, g, c], nmax[u][:, g, c], esum[u][:, g, c], rsum[u][:, g, c], HC)

                        for k in ks:
                            s, m, mx, nm, _, _, n = views(k)
                            dve.wait_ge(s_ready[u], s_ready.at(it, k0 + k + 1))
                            nc.vector.memset(mx, 0.0)
                            link(nc.vector.copy_predicated(s, m, fill[:, L:L + 1].unsqueeze(2).to_broadcast([P, n, P])))
                            link(nc.vector.tensor_reduce(mx, s, AX_X, ALU.max))
                            nc.vector.tensor_scalar(nm, mx, -2.0 if L == 2 else -1.0, scale / 2 if L == 2 else 1.0,
                                                    ALU.mult, ALU.mult).then_inc(max_ready[u], 1)
                        for k in ks:
                            _, _, _, _, es, rs, _ = views(k)
                            dve.wait_ge(exp_ready[u], exp_ready.at(it, k0 + k + 1))
                            if step == "soft0":
                                link(nc.vector.reciprocal(rs, es))
                                nc.vector.tensor_scalar(rs, rs, 1.0 - ALPHA, None, ALU.mult).then_inc(r_ready[u], 1)
                            else:
                                nc.vector.reciprocal(rs, es).then_inc(r_ready[u], 1)
                    if step[:3] == "hop" or step == "pv2":
                        t = int(step[3]) if step[0] == "h" else HOPS
                        for g in range(G):
                            dve.wait_ge(o_t[u], o_t.at(it, G * t + g + 1))
                            o = b[g][:, 0:D].rearrange("p (c n) -> p c n", c=NC)
                            z = zT[u][:, :, g * P:(g + 1) * P]
                            if t < HOPS:
                                a = nc.vector.scalar_tensor_tensor(z, vT[u][:, :, g * P:(g + 1) * P], ALPHA, o,
                                                                   ALU.mult, ALU.add)
                            else:
                                a = nc.vector.tensor_copy(z, o)
                            a.then_inc(zt_ready[u], 1)
                        if t >= HOPS - 1:
                            if t == HOPS:
                                dve.wait_ge(xn_ready[u], xn_ready.at(it, 2))
                            for g in range(G):
                                dve.wait_ge(back[u], back.at(it, (G * t if t < HOPS else G * t + 1) + g + 1))
                                res = x_in[u] if t < HOPS else xnat[u]
                                a = nc.vector.tensor_tensor(y[u][:, g, :], b[2 + g][:, 0:D], res[:, g, :], ALU.add)
                            link(a)
                            if t == HOPS:
                                link(nc.vector.tensor_tensor(y[u][:], y[u][:], rowc("bo2"), ALU.add))
                    if step == "l1b":
                        dve.wait_ge(xn_ready[u], xn_ready.at(it, 1))
                        dve.wait_ge(back[u], back.at(it, 9))
                        link(nc.vector.tensor_tensor(flat(y[u]), b[0][:, :], flat(xnat[u]), ALU.add))
                        link(nc.vector.tensor_tensor(y[u][:], y[u][:], rowc("bo1"), ALU.add))
                    if step[:4] == "norm":
                        L = int(step[-1])
                        layer_norm(u, [y[u][:, g, :] for g in range(G)])
                        dve.wait_ge(xt32[u], xt32.at(it, L))
                        link(nc.vector.tensor_copy(flat(xT_hi[u]), flat(xT[u])))
                        nc.vector.tensor_tensor(flat(xT_lo[u]), flat(xT[u]), flat(xT_hi[u]).bitcast(F32),
                                                ALU.subtract).then_inc(xt_ready[u], 1)
                        if L == 3:
                            for d in range(LABELS):
                                a = nc.vector.tensor_scalar(E[u][:, :, 0, d], adj_f[u][:], float(d + 1), None,
                                                            ALU.is_equal)
                            link(a)
                            for g in range(G):
                                a = nc.vector.tensor_reduce(cnt[u][:, g], E[u][:, g, 0], AX_X, ALU.add)
                            link(a)
                            link(nc.vector.tensor_scalar(cnt[u][:], cnt[u][:], DEG_EPS, None, ALU.add))
                            nc.vector.reciprocal(rcnt[u][:], cnt[u][:]).then_inc(wm_cnt[u], 1)
                    if step == "agg":
                        for k in range(G * NC):
                            g, c = divmod(k, NC)
                            dve.wait_ge(agg_hi_ready[u], agg_hi_ready.at(it, k + 1))
                            nc.vector.tensor_tensor(agg_lo[u][:, c, :, g, :],
                                                    b[k][:, :].rearrange("p (d n) -> p d n", d=LABELS),
                                                    agg_hi[u][:, c, :, g, :].bitcast(F32),
                                                    ALU.subtract).then_inc(agg_lo_ready[u], 1)
                    if step == "out":
                        dve.wait_ge(out32[u], out32.at(it, 1))
                        link(nc.vector.tensor_copy(flat(oT_hi[u]), flat(qT[u])))
                        nc.vector.tensor_tensor(flat(oT_lo[u]), flat(qT[u]), flat(oT_hi[u]).bitcast(F32),
                                                ALU.subtract).then_inc(out_ready[u], 1)
                    if step == "gate":
                        dve.wait_ge(gate_ready[u], gate_ready.at(it, 1))
                        link(nc.vector.tensor_scalar(rT[u][:], rT[u][:], 0.5, 0.5, ALU.mult, ALU.add))
                        for c in range(NC):
                            a = nc.vector.scalar_tensor_tensor(vnat[u][:, c, :], b[3][:, c * GN:(c + 1) * GN],
                                                               colc("bnh", c), rT[u][:, c, :], ALU.add, ALU.mult)
                        link(a)
                        dve.wait_ge(gates[u], gates.at(it, 3))
                        nc.vector.tensor_tensor(flat(vnat[u]), b[0][:, :], flat(vnat[u]), ALU.add)\
                            .then_inc(r_used[u], 1)
                        dve.wait_ge(gate_ready[u], gate_ready.at(it, 2))
                        link(nc.vector.tensor_scalar(vT[u][:], vT[u][:], 0.5, 0.5, ALU.mult, ALU.add))
                        dve.wait_ge(gate_ready[u], gate_ready.at(it, 3))
                        link(nc.vector.tensor_tensor(flat(qT[u]), flat(xT[u]), flat(vnat[u]), ALU.subtract))
                        link(nc.vector.tensor_tensor(flat(qT[u]), flat(qT[u]), flat(vT[u]), ALU.mult))
                        nc.vector.tensor_tensor(flat(qT[u]), flat(qT[u]), flat(vnat[u]), ALU.add)\
                            .then_inc(mixed[u], 1)
                    if step == "fin":
                        dve.wait_ge(mixed_t[u], mixed_t.at(it, 1))
                        layer_norm(u, [b[1][:, g * D:(g + 1) * D] for g in range(G)])
                used = own.used
            assert used == DVE_OWN, used


_OUTS = [((GRAPHS, P, D), "float32")]


def kernel(**inputs):
    import concourse.bacc as _bacc
    from concourse.bass_utils import run_bass_kernel_spmd as _run

    def chunked(w):
        return np.asarray(w).reshape(-1, P, D).transpose(1, 0, 2)

    v = {k: np.asarray(a) for k, a in inputs.items()}
    w = [v[f"L0_gnn_W{n}"].T for n in "qkv"] + [v[f"L2_gnn_W{n}"] for n in "qkv"]
    w += [v["L3_gnn_Wd"].T[D * d:D * d + D] for d in range(LABELS)]
    w += [v[f"L3_gnn_W{n}"].T for n in ("ri", "zi", "ni", "rh", "zh", "nh")]
    l1 = [v["L1_gnn_Wq"].T, v["L1_gnn_Wk"].T, v["L1_gnn_Wv"].T, v["L1_gnn_Wo"]]
    vec = {f"b{n}{L}": v[f"L{L}_gnn_b{n}"] for L in (0, 2) for n in "qkv"}
    vec.update({f"b{n}": v[f"L3_gnn_b{n}"] for n in ("d", "ri", "rh", "zi", "zh", "ni", "nh")})
    vec.update({f"{n}{L}": v[f"L{L}_gnn_{n}"] for L in range(4) for n in ("gamma", "beta")})
    vec.update({f"bo{L}": v[f"L{L}_gnn_bo"] for L in (1, 2)})
    arrays = {
        "x": v["x"],
        "xt": v["x"].transpose(0, 2, 1),
        "adj": v["adj"],
        "weights": np.stack([chunked(a) for a in w], axis=1),
        "l1_weights": np.stack([chunked(a) for a in l1], axis=1),
        "wo2": chunked(v["L2_gnn_Wo"]),
        "cols": np.stack([vec[n].reshape(NC, P) for n in COLS]).reshape(-1, P).T,
        "rows": np.stack([vec[n] for n in ROWS]),
    }
    arrays = {f"in_{k}": np.ascontiguousarray(a) for k, a in arrays.items()}
    nc = _bacc.Bacc("TRN2", target_bir_lowering=False, num_devices=1)
    args = [nc.dram_tensor(n, a.shape, mybir.dt.from_np(a.dtype), kind="ExternalInput").ap()
            for n, a in arrays.items()]
    args += [nc.dram_tensor(f"out_{i}", shape, mybir.dt.from_np(np.dtype(dt)), kind="ExternalOutput").ap()
             for i, (shape, dt) in enumerate(_OUTS)]
    gnn_program(nc, *args)
    r = _run(nc, [arrays], core_ids=[0])
    return r.results[0]["out_0"]
```

```python
from contextlib import ExitStack

import numpy as np
import concourse.bass as bass
from concourse import mybir

P = 128
GRAPHS = 64
D = 256
NC = D // P
HEADS = 8
HD = D // HEADS
HC = P // HD
LABELS = 4
G = 2
UNITS = 2
ROUNDS = GRAPHS // (G * UNITS)
GN = G * P
LN_EPS = 1e-5
DEG_EPS = 1e-8
ALPHA = 0.1
HOPS = 4

ALU = mybir.AluOpType
ACT = mybir.ActivationFunctionType
AX_X = mybir.AxisListType.X
F32 = mybir.dt.float32
F32R = mybir.dt.float32r
I32 = mybir.dt.int32
BF16 = mybir.dt.bfloat16

SLOTS = ["q0", "k0", "v0", "q2", "k2", "v2", "d0", "d1", "d2", "d3",
         "ri", "zi", "ni", "rh", "zh", "nh"]
LOADED = len(SLOTS)
SLOT = {n: i for i, n in enumerate(SLOTS + ["g1", "vo1"])}
COLS = ["bq0", "bk0", "bv0", "bq2", "bk2", "bv2", "bd", "bri", "brh", "bzi", "bzh", "bni", "bnh",
        "gamma0", "beta0", "gamma1", "beta1", "gamma2", "beta2"]
COL = {n: NC * i for i, n in enumerate(COLS)}
ROWS = ["gamma0", "beta0", "gamma1", "beta1", "gamma2", "beta2", "gamma3", "beta3", "bo1", "bo2"]
ROW = {n: i for i, n in enumerate(ROWS)}


def by(n, *steps):
    return [(s, p) for s in steps for p in range(n)]


SB = G * NC
HOP_STEPS = [s for t in range(HOPS) for s in (f"hop{t}", f"back{t}")]
PIECES = {
    "tensor": by(3, "qkv0") + by(1, "kv0") + by(SB, "score0", "pt0") + by(G, *HOP_STEPS)
    + by(1, "nrm1") + by(2, "proj1") + by(1, "score1", "pt1", "y1", "nrm2")
    + by(3, "qkv2") + by(1, "kv2") + by(SB, "score2", "pt2") + by(G, "hop4", "back4") + by(1, "nrm3")
    + by(G, "wt") + by(SB, "agg") + by(NC, "out") + by(1, "osplit") + by(3, "gate") + by(1, "mixt"),
    "scalar": by(1, "in") + by(3, "qkv0") + by(1, "kv0") + by(SB, "exp0", "pt0") + by(G, "back0", "back1", "back2")
    + by(1, "nrm1") + by(2, "proj1") + by(1, "exp1", "pt1", "nrm2")
    + by(3, "qkv2") + by(1, "kv2") + by(SB, "exp2", "pt2") + by(1, "nrm3")
    + by(G, "wt") + by(SB, "agg") + by(1, "out") + by(2, "gate") + by(1, "mix"),
    "gpsimd": by(1, "in") + by(SB, "exp0") + by(1, "stat1", "nrm1", "exp1", "stat2", "nrm2") + by(SB, "exp2")
    + by(1, "stat3", "mask", "nrm3", "stat4", "last"),
    "vector": by(1, "in", "kv0") + by(SB, "score0", "exp0")
    + by(G, "hop0", "hop1", "hop2", "hop3", "back3") + by(1, "stat1", "nrm1", "split1")
    + by(1, "score1", "exp1", "y1", "stat2", "nrm2", "split2", "kv2") + by(SB, "score2", "exp2")
    + by(G, "hop4", "back4") + by(1, "stat3", "mask", "nrm3", "split3")
    + by(SB, "agg") + by(1, "osplit") + by(2, "gate", "mix") + by(1, "stat4", "last"),
    "sync": by(1, "nrm1", "last"),
}

TURNS = {
    "tensor": (38, [0, 5, 3, 2, 2, 1, 2, 1, 1, 4, 7, 1, 7, 1, 2, 1, 4, 3, 1, 1, 3, 1, 1, 2, 1, 2, 1, 1, 3, 1,
                   5, 3, 2, 4, 3, 1, 3, 9, 1, 6, 2, 2, 3, 2, 1, 1, 1, 1, 1, 3, 1, 2, 2, 1, 1, 3, 1]),
    "scalar": (25, [0, 3, 1, 4, 3, 4, 1, 1, 10, 1, 4, 5, 2, 1, 3, 2, 1, 2, 3, 1, 4, 3, 2, 1, 3, 10, 1, 3, 3, 1,
                   3, 1, 1, 4, 1, 1, 2]),
    "gpsimd": (10, [0, 3, 1, 1, 4, 3, 5, 2, 2, 1, 2, 4, 3, 5, 2]),
    "vector": (31, [0, 1, 1, 5, 1, 1, 3, 2, 3, 2, 1, 1, 1, 2, 4, 1, 9, 4, 2, 1, 3, 1, 1, 3, 1, 1, 1, 1, 1, 1,
                   4, 1, 2, 3, 1, 2, 1, 1, 1, 1, 1, 1, 2, 2, 1, 2, 1, 2, 1, 1, 1, 1, 1, 2, 1, 5, 1, 3, 1, 1, 3,
                   1, 1, 1, 1]),
    "sync": (1, [1, 2, 1]),
}


def merged(engine):
    pieces = PIECES[engine]
    at, runs = TURNS[engine]
    order, i, j = [], 0, at
    for k, n in enumerate(runs):
        for _ in range(n):
            if k % 2 == 0:
                order.append((*pieces[i], 0, 0))
                i += 1
            else:
                order.append((*pieces[j % len(pieces)], 1, int(j < len(pieces) and at > 0)))
                j += 1
    assert i == j - at == len(pieces), (engine, i, j)
    return order


def passes(eng, engine):
    order = merged(engine)
    yield 0, [x for x in order if x[-1] == 0]
    with eng.Fori(1, ROUNDS) as it:
        yield it, order
    yield ROUNDS, [x for x in order if x[-1] == 1]


class Signal:

    def __init__(self, sems, per_round):
        self.sem, self.per_round = sems, per_round

    def __getitem__(self, u):
        return self.sem[u]

    def at(self, it, k):
        return it * self.per_round + k


class Own:

    def __init__(self, sems, per_round):
        self.sem, self.per_round, self.used = sems, per_round, [0] * len(sems)

    def next(self, it, u):
        self.used[u] += 1
        return it * self.per_round + self.used[u]

    def start(self, u, n=0):
        assert self.used[u] in (0, self.per_round), self.used
        self.used[u] = n


DVE_OWN = 38
POOL_OWN = 4


def gnn_program(nc, x, xt, adj, weights, l1_weights, wo2, cols, rows, out):
    ctx = ExitStack()
    with ctx:
        def sb(name, shape, dt=F32):
            return ctx.enter_context(nc.sbuf_tensor(name, shape, dt))

        def sem(name):
            return ctx.enter_context(nc.semaphore(name))

        def per_unit(name, shape, dt=F32):
            return [sb(f"{name}_{u}", shape, dt) for u in range(UNITS)]

        def aliased(name, over, shape, dt):
            return [nc.alloc_sbuf_tensor_at(f"{name}_{u}", shape, dt, offset=nc.lookup_mloc(over[u]).addr) for u in range(UNITS)]

        ident = sb("ident", [P, P])
        ident_b = sb("ident_b", [P, P], BF16)
        w_hi = sb("w_hi", [P, len(SLOT), NC, D], F32R)
        w_lo = sb("w_lo", [P, len(SLOT), NC, D], F32R)
        wo2_sb = sb("wo2_sb", [P, NC, D])
        col = sb("col", [P, NC * len(COLS)])
        half = sb("half", [P, 2 * NC])
        row = sb("row", [P, len(ROWS), D])
        fill = sb("fill", [P, 1])
        minus_half = sb("minus_half", [P, G])
        pidle = sb("pidle", [P, 1])
        psink = [sb(f"psink_{u}", [P, 1]) for u in range(2)]

        x_in = per_unit("x_in", [P, G, D])
        xt_in = per_unit("xt_in", [P, NC, G, P])
        adj_in = per_unit("adj_in", [P, G, P], I32)
        absent = per_unit("absent", [P, G, P], I32)
        no_edge = per_unit("no_edge", [P, G, P], BF16)
        adj_f = per_unit("adj_f", [P, G, P])
        xT = per_unit("xT", [P, NC, GN])
        xT_hi = per_unit("xT_hi", [P, NC, GN], F32R)
        xT_lo = per_unit("xT_lo", [P, NC, GN], F32R)
        xnat = per_unit("xnat", [P, G, D])
        y = per_unit("y", [P, G, D])
        qT = per_unit("qT", [P, NC, GN])
        kT = per_unit("kT", [P, NC, GN])
        vT = per_unit("vT", [P, NC, GN])
        vnat = per_unit("vnat", [P, G, D])
        kblk = per_unit("kblk", [P, NC, G, HC, P])
        E = per_unit("E", [P, G, NC, HC, P])
        PT = per_unit("PT", [P, G, NC, HC, P])
        wT = per_unit("wT", [P, G, LABELS, P])
        oT_hi = per_unit("oT_hi", [P, NC, GN], F32R)
        oT_lo = per_unit("oT_lo", [P, NC, GN], F32R)
        nmax = per_unit("nmax", [P, G, NC, HC])
        rmax = per_unit("rmax", [P, G, NC, HC])
        esum = per_unit("esum", [P, G, NC, HC])
        rsum = per_unit("rsum", [P, G, NC, HC])
        cnt = per_unit("cnt", [P, G, LABELS])
        rcnt = per_unit("rcnt", [P, G, LABELS])
        stats = per_unit("stats", [P, G, 6])
        mv = per_unit("mv", [P, G, 2])
        var = per_unit("var", [P, G])
        rstd = per_unit("rstd", [P, G])
        zT, rT = kT, kT
        agg_hi = aliased("agg_hi", E, [P, NC, LABELS, G, P], F32R)
        agg_lo = aliased("agg_lo", PT, [P, NC, LABELS, G, P], F32R)

        ps = [[ctx.enter_context(nc.psum_tensor(f"bank_{u}_{b}", [P, 512], F32)) for b in range(4)]
              for u in range(UNITS)]

        def signal(name, per_round):
            return Signal([sem(f"{name}_{u}") for u in range(UNITS)], per_round)

        loaded = signal("loaded", 4 * 16)
        adj_ready = signal("adj_ready", 2)
        x0_hi = signal("x0_hi", 1)
        xt32 = signal("xt32", 3)
        xt_ready = signal("xt_ready", 4)
        proj = signal("proj", 8)
        q_ready = signal("q_ready", 3)
        k_ready = signal("k_ready", 2)
        kblk_ready = signal("kblk_ready", 2)
        v_ready = signal("v_ready", 2)
        vback = signal("vback", 2)
        vn_ready = signal("vn_ready", 3)
        s_ready = signal("s_ready", 9)
        max_ready = signal("max_ready", 9)
        exp_ready = signal("exp_ready", 9)
        r_ready = signal("r_ready", 9)
        e_ready = signal("e_ready", 9)
        p_t = signal("p_t", 9)
        pt_ready = signal("pt_ready", 9)
        o_t = signal("o_t", 10)
        zt_ready = signal("zt_ready", 10)
        back = signal("back", 11)
        z_ready = signal("z_ready", 6)
        var_ready = signal("var_ready", 4)
        rstd_ready = signal("rstd_ready", 4)
        nrm_ready = signal("nrm_ready", 4)
        n_t = signal("n_t", 3)
        xn_ready = signal("xn_ready", 4)
        wm_cnt = signal("wm_cnt", 1)
        wm_ready = signal("wm_ready", 1)
        w_t = signal("w_t", 2)
        wt_ready = signal("wt_ready", 2)
        agg = signal("agg", 4)
        agg_hi_ready = signal("agg_hi_ready", 4)
        agg_lo_ready = signal("agg_lo_ready", 4)
        out_t = signal("out_t", 1)
        out32 = signal("out32", 1)
        out_ready = signal("out_ready", 1)
        gates = signal("gates", 3)
        gate_ready = signal("gate_ready", 3)
        r_used = signal("r_used", 1)
        mixed = signal("mixed", 1)
        mixed_t = signal("mixed_t", 1)
        stored = signal("stored", 16)

        w_loaded = [sem(f"w_loaded_{j}") for j in range(LOADED // 4 + 1)]
        c_loaded, w_split, w_read, l1_prod, consts = (
            sem(n) for n in ("c_loaded", "w_split", "w_read", "l1_prod", "consts"))
        wmade = sem("wmade")
        dve_own = Own([sem(f"dve_own_{u}") for u in range(UNITS)], DVE_OWN)
        pool_own = Own([sem(f"pool_own_{u}") for u in range(UNITS)], POOL_OWN)
        dve_pre, pool_pre = sem("dve_pre"), sem("pool_pre")

        UR = range(UNITS)
        x_v = x.rearrange("(r u g) n d -> r u n g d", u=UNITS, g=G)
        xt_v = xt.rearrange("(r u g) (c p) n -> r u p c g n", u=UNITS, g=G, p=P)
        adj_v = adj.rearrange("(r u g) n m -> r u n g m", u=UNITS, g=G)
        out_v = out.rearrange("(r u g) n d -> r u n g d", u=UNITS, g=G)

        def rowc(name, n=G):
            return row[:, ROW[name]:ROW[name] + 1, :].to_broadcast([P, n, D])

        def colc(name, c):
            return col[:, COL[name] + c:COL[name] + c + 1]

        def flat(t):
            return t[:].rearrange("p a b -> p (a b)")

        stage = [kblk[j][:].rearrange("p c g h n -> p (c g h n)").rearrange("p (s c d) -> p s c d", s=4, c=NC)
                 for j in UR]
        WR = LOADED // 4
        block = ctx.enter_context(nc.Block())

        @block.sync
        def _(sp):
            sp.dma_start(col[:], cols).then_inc(c_loaded, 16)
            sp.dma_start(row[:], rows.unsqueeze(0).to_broadcast([P, len(ROWS), D])).then_inc(c_loaded, 16)
            sp.dma_start(wo2_sb[:], wo2).then_inc(c_loaded, 16)
            for j in range(WR):
                if j >= 2:
                    sp.wait_ge(w_split, j - 1)
                sp.dma_start(stage[j % 2], weights[:, 4 * j:4 * j + 4]).then_inc(w_loaded[j], 16)
            sp.wait_ge(w_split, WR - 1)
            sp.dma_start(stage[WR % 2], l1_weights).then_inc(w_loaded[WR], 16)

            def load(r, u):
                sp.dma_start(x_in[u][:], x_v[r, u]).then_inc(loaded[u], 16)
                for c in range(NC):
                    sp.dma_start(xt_in[u][:, c], xt_v[r, u][:, c]).then_inc(loaded[u], 16)
                sp.dma_start(adj_in[u][:], adj_v[r, u]).then_inc(loaded[u], 16)

            def store(r, u, it):
                sp.wait_ge(xn_ready[u], xn_ready.at(it, 4))
                sp.dma_start(out_v[r, u], xnat[u][:]).then_inc(stored[u], 16)

            for u in UR:
                load(0, u)

            def moves(now, order):
                for step, _, u, lag in order:
                    it = now - lag
                    if step == "nrm1" and not (isinstance(it, int) and it + 1 >= ROUNDS):
                        sp.wait_ge(adj_ready[u], adj_ready.at(it, 2))
                        sp.wait_ge(nrm_ready[u], nrm_ready.at(it, 1))
                        load(it + 1, u)
                    if step == "last":
                        store(it, u, it)

            order = merged("sync")
            moves(0, [x for x in order if x[-1] == 0])
            with sp.Fori(1, ROUNDS - 1) as now:
                moves(now, order)
            moves(ROUNDS - 1, order)
            moves(ROUNDS, [x for x in order if x[-1] == 1])
            for u in UR:
                sp.wait_ge(stored[u], stored.at(ROUNDS, 16))

        @block.tensor
        def _(pe):
            def split_product(o, w, n, xh, xl, first, last, count=1):
                for kc in range(NC):
                    for j, (a, b) in enumerate(((w_hi, xh), (w_hi, xl), (w_lo, xh))):
                        mm = nc.tensor.matmul(o[0], a[:, n, kc, o[1] * P:(o[1] + 1) * P], b(kc),
                                              start=first and kc == 0 and j == 0,
                                              stop=last and kc == NC - 1 and j == 2)
                return mm

            def project(bank, names, ocs=range(NC)):
                for oc in ocs:
                    for i, (n, hi, lo) in enumerate(names):
                        mm = split_product((bank[:, oc * GN:(oc + 1) * GN], oc), None, SLOT[n], hi, lo,
                                           i == 0, i == len(names) - 1)
                return mm

            pe.wait_ge(w_loaded[WR], 16)
            s = stage[WR % 2]
            for b, (i, j) in enumerate(((0, 1), (2, 3))):
                for kc in range(NC):
                    for jc in range(NC):
                        mm = nc.tensor.matmul(ps[0][b][:, kc * D:(kc + 1) * D], s[:, i, jc, kc * P:(kc + 1) * P],
                                              s[:, j, jc, :], start=jc == 0, stop=jc == NC - 1)
                mm.then_inc(l1_prod, 1)
            pe.wait_ge(wmade, 1)

            for now, order in passes(pe, "tensor"):
                def x_parts(u):
                    return (lambda kc: xT_hi[u][:, kc, :], lambda kc: xT_lo[u][:, kc, :])

                for step, part, u, lag in order:
                    it, b = now - lag, ps[u]
                    if step in ("qkv0", "qkv2"):
                        L = int(step[-1])
                        if part == 0:
                            pe.wait_ge(xt_ready[u], xt_ready.at(it, L + 1))
                        project(b[part], [(f"{'qkv'[part]}{L}", *x_parts(u))]).then_inc(proj[u], 1)
                    if step in ("kv0", "kv2"):
                        a = int(step[-1]) // 2
                        pe.wait_ge(v_ready[u], v_ready.at(it, a + 1))
                        for g in range(G):
                            for c in range(NC):
                                mm = nc.tensor.transpose(b[3][:, (g * NC + c) * P:(g * NC + c + 1) * P],
                                                         vT[u][:, c, g * P:(g + 1) * P], ident[:])
                        mm.then_inc(vback[u], 1)
                    if step in ("score0", "score2"):
                        L = int(step[-1])
                        a = L // 2
                        k = part
                        g, c = divmod(k, NC)
                        if k == 0:
                            pe.wait_ge(q_ready[u], q_ready.at(it, L + 1))
                            pe.wait_ge(kblk_ready[u], kblk_ready.at(it, a + 1))
                        if k == 3:
                            pe.wait_ge(vn_ready[u], vn_ready.at(it, L + 1))
                        mm = nc.tensor.matmul(b[k][:, :], qT[u][:, c, g * P:(g + 1) * P],
                                              kblk[u][:, c, g].rearrange("p h n -> p (h n)"),
                                              start=True, stop=L == 0)
                        if L == 2:
                            mm = nc.tensor.matmul(b[k][:, :], ident_b[:],
                                                  no_edge[u][:, g:g + 1, :].to_broadcast([P, HC, P]),
                                                  start=False, stop=True)
                        mm.then_inc(s_ready[u], 1)
                    if step in ("pt0", "pt2"):
                        k0 = 0 if step == "pt0" else 5
                        k = part
                        g, c = divmod(k, NC)
                        pe.wait_ge(e_ready[u], e_ready.at(it, k0 + k + 1))
                        for h in range(HC):
                            mm = nc.tensor.transpose(b[k][:, h * P:(h + 1) * P], E[u][:, g, c, h], ident[:])
                        mm.then_inc(p_t[u], 1)
                    if step[:3] == "hop":
                        t = int(step[3])
                        if t in (0, HOPS) and part == 0:
                            pe.wait_ge(pt_ready[u], pt_ready.at(it, 4 if t == 0 else 9))
                        for g in [part]:
                            if 0 < t < HOPS:
                                pe.wait_ge(z_ready[u], z_ready.at(it, G * (t - 1) + g + 1))
                            for h in range(HEADS):
                                c, hh = divmod(h, HC)
                                mm = nc.tensor.matmul(b[g][hh * HD:(hh + 1) * HD, c * P:(c + 1) * P],
                                                      vnat[u][:, g, h * HD:(h + 1) * HD], PT[u][:, g, c, hh],
                                                      start=True, stop=True)
                            mm.then_inc(o_t[u], 1)
                    if step[:4] == "back":
                        t = int(step[4])
                        for g in [part]:
                            pe.wait_ge(zt_ready[u], zt_ready.at(it, G * t + g + 1))
                            for c in range(NC):
                                zc = zT[u][:, c, g * P:(g + 1) * P]
                                if t < HOPS:
                                    mm = nc.tensor.transpose(b[2 + g][:, c * P:(c + 1) * P], zc, ident[:])
                                else:
                                    mm = nc.tensor.matmul(b[2 + g][:, 0:D], zc, wo2_sb[:, c, :],
                                                          start=c == 0, stop=c == NC - 1)
                            mm.then_inc(back[u], 1)
                    if step in ("nrm1", "nrm2", "nrm3"):
                        L = int(step[-1])
                        pe.wait_ge(nrm_ready[u], nrm_ready.at(it, L))
                        for c in range(NC):
                            for g in range(G):
                                mm = nc.tensor.transpose(b[0][:, c * GN + g * P:c * GN + (g + 1) * P],
                                                         y[u][:, g, c * P:(c + 1) * P], ident[:])
                        mm.then_inc(n_t[u], 1)
                    if step == "proj1" and part == 0:
                        pe.wait_ge(xt_ready[u], xt_ready.at(it, 2))
                        project(b[0], [("g1", *x_parts(u))]).then_inc(proj[u], 1)
                    if step == "proj1" and part == 1:
                        n = SLOT["vo1"]
                        for g in range(G):
                            for c in range(NC):
                                xs = slice(g * P, (g + 1) * P)
                                for j, (a, w) in enumerate(((xT_hi, w_hi), (xT_lo, w_hi), (xT_hi, w_lo))):
                                    mm = nc.tensor.matmul(b[1][:, g * D:(g + 1) * D], a[u][:, c, xs], w[:, n, c, :],
                                                          start=c == 0 and j == 0, stop=c == NC - 1 and j == 2)
                        mm.then_inc(proj[u], 1)
                    if step == "score1":
                        pe.wait_ge(q_ready[u], q_ready.at(it, 2))
                        for g in range(G):
                            for c in range(NC):
                                xs = slice(g * P, (g + 1) * P)
                                nc.tensor.matmul(b[2][:, g * P:(g + 1) * P], qT[u][:, c, xs], xT[u][:, c, xs],
                                                 start=c == 0, stop=False)
                            mm = nc.tensor.matmul(b[2][:, g * P:(g + 1) * P], ident_b[:], no_edge[u][:, g, :],
                                                  start=False, stop=True)
                        mm.then_inc(s_ready[u], 1)
                    if step == "pt1":
                        pe.wait_ge(e_ready[u], e_ready.at(it, 5))
                        for g in range(G):
                            mm = nc.tensor.transpose(b[3][:, g * P:(g + 1) * P], E[u][:, g, 0, 0], ident[:])
                        mm.then_inc(p_t[u], 1)
                    if step == "y1":
                        pe.wait_ge(pt_ready[u], pt_ready.at(it, 5))
                        pe.wait_ge(vn_ready[u], vn_ready.at(it, 2))
                        for g in range(G):
                            mm = nc.tensor.matmul(b[0][:, g * D:(g + 1) * D], PT[u][:, g, 0, 0], vnat[u][:, g, :],
                                                  start=True, stop=True)
                        mm.then_inc(back[u], 1)
                    if step == "wt":
                        if part == 0:
                            pe.wait_ge(wm_ready[u], wm_ready.at(it, 1))
                            pe.wait_ge(xt_ready[u], xt_ready.at(it, 4))
                        for g in [part]:
                            for d in range(LABELS):
                                mm = nc.tensor.transpose(b[g][:, d * P:(d + 1) * P], E[u][:, g, 0, d], ident[:])
                            mm.then_inc(w_t[u], 1)
                    if step == "agg":
                        g, c = divmod(part, NC)
                        if part == 0:
                            pe.wait_ge(xn_ready[u], xn_ready.at(it, 3))
                            pe.wait_ge(wt_ready[u], wt_ready.at(it, 2))
                        nc.tensor.matmul(b[part][:, :], xnat[u][:, g, c * P:(c + 1) * P],
                                         wT[u][:, g].rearrange("p d n -> p (d n)"),
                                         start=True, stop=True).then_inc(agg[u], 1)
                    if step == "out":
                        if part == 0:
                            pe.wait_ge(agg_lo_ready[u], agg_lo_ready.at(it, 4))
                        mm = project(b[0], [(f"d{d}",
                                             (lambda kc, d=d: agg_hi[u][:, kc, d].rearrange("p g n -> p (g n)")),
                                             (lambda kc, d=d: agg_lo[u][:, kc, d].rearrange("p g n -> p (g n)")))
                                            for d in range(LABELS)], [part])
                        if part == NC - 1:
                            mm.then_inc(out_t[u], 1)
                    if step == "osplit":
                        project(b[3], [("nh", *x_parts(u))])
                    if step == "gate":
                        o_parts = (lambda kc: oT_hi[u][:, kc, :], lambda kc: oT_lo[u][:, kc, :])
                        if part == 0:
                            pe.wait_ge(out_ready[u], out_ready.at(it, 1))
                        bank, names = ((b[1], ("rh", "ri")), (b[2], ("zh", "zi")), (b[0], ("ni",)))[part]
                        project(bank, [(n, *(x_parts(u) if n[1] == "h" else o_parts)) for n in names])\
                            .then_inc(gates[u], 1)
                    if step == "mixt":
                        pe.wait_ge(mixed[u], mixed.at(it, 1))
                        for g in range(G):
                            for c in range(NC):
                                mm = nc.tensor.transpose(b[1][:, g * D + c * P:g * D + (c + 1) * P],
                                                         qT[u][:, c, g * P:(g + 1) * P], ident[:])
                        mm.then_inc(mixed_t[u], 1)

        @block.scalar
        def _(act):
            for j in range(WR):
                act.wait_ge(w_loaded[j], 16)
                nc.scalar.activation(w_hi[:, 4 * j:4 * j + 4].rearrange("p s c d -> p (s c d)"),
                                     stage[j % 2].rearrange("p s c d -> p (s c d)"), ACT.Copy).then_inc(w_read, 1)
            for b, (n, scale) in enumerate((("g1", float(D) ** -0.5), ("vo1", 1.0))):
                act.wait_ge(l1_prod, b + 1)
                nc.scalar.activation(w_hi[:, SLOT[n]].rearrange("p c d -> p (c d)"), ps[0][b][:, :], ACT.Copy,
                                     scale=scale).then_inc(w_read, 1)
            act.wait_ge(wmade, 1)
            for now, order in passes(act, "scalar"):
                for step, part, u, lag in order:
                    it, b = now - lag, ps[u]
                    if step == "in":
                        act.wait_ge(loaded[u], loaded.at(it, 64))
                        nc.scalar.activation(adj_f[u][:], adj_in[u][:], ACT.Copy)
                        nc.scalar.activation(flat(xT_hi[u]), xt_in[u][:].rearrange("p c g n -> p (c g n)"),
                                             ACT.Copy).then_inc(x0_hi[u], 1)
                    if step in ("qkv0", "qkv2"):
                        L = int(step[-1])
                        p0 = 0 if L == 0 else 5
                        n, t, ready = (("q", qT, q_ready), ("k", kT, k_ready), ("v", vT, v_ready))[part]
                        act.wait_ge(proj[u], proj.at(it, p0 + part + 1))
                        for c in range(NC):
                            a = nc.scalar.activation(t[u][:, c, :], b[part][:, c * GN:(c + 1) * GN], ACT.Identity,
                                                     bias=colc(f"b{n}{L}", c))
                        a.then_inc(ready[u], 1)
                    if step in ("kv0", "kv2"):
                        act.wait_ge(vback[u], vback.at(it, int(step[-1]) // 2 + 1))
                        nc.scalar.activation(flat(vnat[u]), b[3][:, :], ACT.Copy).then_inc(vn_ready[u], 1)
                    if step in ("exp0", "exp2"):
                        k0 = 0 if step == "exp0" else 5
                        scale = 1.0 if step == "exp0" else float(HD) ** -0.5
                        for k in [part]:
                            g, c = divmod(k, NC)
                            act.wait_ge(max_ready[u], max_ready.at(it, k0 + k + 1))
                            for h in range(HC):
                                a = nc.scalar.activation(E[u][:, g, c, h], b[k][:, h * P:(h + 1) * P], ACT.Exp,
                                                         bias=nmax[u][:, g, c, h:h + 1], scale=scale,
                                                         accum_out=esum[u][:, g, c, h:h + 1])
                            a.then_inc(exp_ready[u], 1)
                    if step in ("pt0", "pt2"):
                        k0 = 0 if step == "pt0" else 5
                        for k in [part]:
                            g, c = divmod(k, NC)
                            act.wait_ge(p_t[u], p_t.at(it, k0 + k + 1))
                            nc.scalar.activation(PT[u][:, g, c].rearrange("p h n -> p (h n)"), b[k][:, :],
                                                 ACT.Copy, scale=1.0 - ALPHA if k0 == 0 else 1.0)\
                                .then_inc(pt_ready[u], 1)
                    if step in ("back0", "back1", "back2"):
                        t = int(step[4])
                        for g in [part]:
                            act.wait_ge(back[u], back.at(it, G * t + g + 1))
                            nc.scalar.activation(vnat[u][:, g, :], b[2 + g][:, 0:D], ACT.Copy).then_inc(z_ready[u], 1)
                    if step in ("nrm1", "nrm2", "nrm3"):
                        L = int(step[-1])
                        act.wait_ge(n_t[u], n_t.at(it, L))
                        for c in range(NC):
                            a = nc.scalar.activation(xT[u][:, c, :], b[0][:, c * GN:(c + 1) * GN], ACT.Identity,
                                                     bias=colc(f"beta{L - 1}", c), scale=colc(f"gamma{L - 1}", c))
                        a.then_inc(xt32[u], 1)
                    if step == "proj1":
                        to, ready = ((qT, q_ready), (vnat, vn_ready))[part]
                        act.wait_ge(proj[u], proj.at(it, 4 + part))
                        nc.scalar.activation(flat(to[u]), b[part][:, :], ACT.Copy).then_inc(ready[u], 1)
                    if step == "exp1":
                        act.wait_ge(max_ready[u], max_ready.at(it, 5))
                        for g in range(G):
                            a = nc.scalar.activation(E[u][:, g, 0, 0], b[2][:, g * P:(g + 1) * P], ACT.Exp,
                                                     bias=nmax[u][:, g, 0, 0:1], accum_out=esum[u][:, g, 0, 0:1])
                        a.then_inc(exp_ready[u], 1)
                    if step == "pt1":
                        act.wait_ge(p_t[u], p_t.at(it, 5))
                        nc.scalar.activation(PT[u][:, :, 0, 0], b[3][:, 0:GN].rearrange("p (g n) -> p g n", g=G),
                                             ACT.Copy).then_inc(pt_ready[u], 1)
                    if step == "wt":
                        for g in [part]:
                            act.wait_ge(w_t[u], w_t.at(it, g + 1))
                            nc.scalar.activation(wT[u][:, g].rearrange("p d n -> p (d n)"), b[g][:, :],
                                                 ACT.Copy).then_inc(wt_ready[u], 1)
                    if step == "agg":
                        for k in [part]:
                            g, c = divmod(k, NC)
                            act.wait_ge(agg[u], agg.at(it, k + 1))
                            nc.scalar.activation(agg_hi[u][:, c, :, g, :],
                                                 b[k][:, :].rearrange("p (d n) -> p d n", d=LABELS),
                                                 ACT.Copy).then_inc(agg_hi_ready[u], 1)
                    if step == "out":
                        act.wait_ge(out_t[u], out_t.at(it, 1))
                        for c in range(NC):
                            a = nc.scalar.activation(qT[u][:, c, :], b[0][:, c * GN:(c + 1) * GN], ACT.Relu,
                                                     bias=colc("bd", c))
                        a.then_inc(out32[u], 1)
                    if step == "gate":
                        for i, t in ((part, (rT, vT)[part]),):
                            act.wait_ge(gates[u], gates.at(it, i + 1))
                            for c in range(NC):
                                a = nc.scalar.activation(t[u][:, c, :], b[i + 1][:, c * GN:(c + 1) * GN], ACT.Tanh,
                                                         bias=half[:, NC * i + c:NC * i + c + 1], scale=0.5)
                            a.then_inc(gate_ready[u], 1)
                    if step == "mix":
                        act.wait_ge(r_used[u], r_used.at(it, 1))
                        for c in range(NC):
                            v = vnat[u][:, c, :]
                            a = nc.scalar.activation(v, v, ACT.Tanh, bias=colc("bni", c))
                        a.then_inc(gate_ready[u], 1)

        @block.gpsimd
        def _(pool):
            own = pool_own

            nc.gpsimd.memset(pidle[:], 0.0)
            nc.gpsimd.memset(ident[:], 0.0).then_inc(pool_pre, 1)
            pool.wait_ge(pool_pre, 1)
            nc.gpsimd.affine_select(out=ident[:], in_=ident[:], compare_op=ALU.not_equal, fill=1.0, base=0,
                                    pattern=[[-1, P]], channel_multiplier=1).then_inc(consts, 1)
            for u in UR:
                pool.sem_inc(stored[u], 16)
            pool.wait_ge(wmade, 1)
            for now, order in passes(pool, "gpsimd"):
                def scale_shift(u, gamma, beta):
                    nc.gpsimd.tensor_tensor(xnat[u][:], y[u][:], rowc(gamma), ALU.mult).then_inc(own.sem[u], 1)
                    pool.wait_ge(own.sem[u], own.next(it, u))
                    return nc.gpsimd.tensor_tensor(xnat[u][:], xnat[u][:], rowc(beta), ALU.add)

                for step, part, u, lag in order:
                    it, b = now - lag, ps[u]
                    if step == "in":
                        own.start(u)
                        pool.wait_ge(loaded[u], loaded.at(it, 64))
                        nc.gpsimd.tensor_tensor(psink[u][:], pidle[:], pidle[:], ALU.mult)
                        nc.gpsimd.tensor_scalar(absent[u][:], adj_in[u][:], 0.0, None, ALU.is_equal)\
                            .then_inc(adj_ready[u], 1)
                        nc.gpsimd.tensor_scalar(no_edge[u][:], adj_in[u][:], 0.0, -3e38, ALU.is_equal, ALU.mult)\
                            .then_inc(adj_ready[u], 1)
                    if step in ("exp0", "exp1", "exp2"):
                        k0 = {"exp0": 0, "exp1": 4, "exp2": 5}[step]
                        for k in [part]:
                            g, c = divmod(k, NC)
                            pool.wait_ge(r_ready[u], r_ready.at(it, k0 + k + 1))
                            if step == "exp1":
                                e, r = E[u][:, :, 0, 0], rsum[u][:, :, 0, 0:1].to_broadcast([P, G, P])
                            else:
                                e, r = E[u][:, g, c], rsum[u][:, g, c].unsqueeze(2).to_broadcast([P, HC, P])
                            nc.gpsimd.tensor_tensor(e, e, r, ALU.mult).then_inc(e_ready[u], 1)
                    if step in ("stat1", "stat2", "stat3", "stat4"):
                        pool.wait_ge(var_ready[u], var_ready.at(it, int(step[-1])))
                        nc.gpsimd.tensor_tensor(rstd[u][:], var[u][:], minus_half[:], ALU.pow)\
                            .then_inc(rstd_ready[u], 1)
                    if step in ("nrm1", "nrm2", "nrm3"):
                        L = int(step[-1])
                        pool.wait_ge(nrm_ready[u], nrm_ready.at(it, L))
                        if L == 1:
                            pool.wait_ge(stored[u], stored.at(it, 16))
                        scale_shift(u, f"gamma{L - 1}", f"beta{L - 1}").then_inc(xn_ready[u], 1)
                    if step == "mask":
                        pool.wait_ge(wm_cnt[u], wm_cnt.at(it, 1))
                        for g in range(G):
                            w = E[u][:, g, 0]
                            a = nc.gpsimd.tensor_tensor(w, w, rcnt[u][:, g].unsqueeze(2).to_broadcast([P, LABELS, P]),
                                                        ALU.mult)
                        a.then_inc(wm_ready[u], 1)
                    if step == "last":
                        pool.wait_ge(nrm_ready[u], nrm_ready.at(it, 4))
                        scale_shift(u, "gamma3", "beta3").then_inc(xn_ready[u], 1)
            assert own.used == [POOL_OWN] * UNITS, own.used

        @block.vector
        def _(dve):
            own = dve_own
            pre = [0]

            def settle(ins):
                pre[0] += 1
                ins.then_inc(dve_pre, 1)
                dve.wait_ge(dve_pre, pre[0])

            nc.vector.memset(fill[:], -16384.0)
            dve.wait_ge(c_loaded, 48)
            for i, n in enumerate("rz"):
                for c in range(NC):
                    settle(nc.vector.tensor_tensor(half[:, NC * i + c:NC * i + c + 1], colc(f"b{n}i", c),
                                                   colc(f"b{n}h", c), ALU.add))
            settle(nc.vector.tensor_scalar(half[:], half[:], 0.5, None, ALU.mult))
            for j in range(WR):
                dve.wait_ge(w_read, j + 1)
                nc.vector.tensor_tensor(w_lo[:, 4 * j:4 * j + 4].rearrange("p s c d -> p (s c d)"),
                                        stage[j % 2].rearrange("p s c d -> p (s c d)"),
                                        w_hi[:, 4 * j:4 * j + 4].bitcast(F32).rearrange("p s c d -> p (s c d)"),
                                        ALU.subtract).then_inc(w_split, 1)
            for b, (n, scale) in enumerate((("g1", float(D) ** -0.5), ("vo1", 1.0))):
                dve.wait_ge(w_read, WR + b + 1)
                settle(nc.vector.scalar_tensor_tensor(w_lo[:, SLOT[n]].rearrange("p c d -> p (c d)"), ps[0][b][:, :],
                                                      scale, w_hi[:, SLOT[n]].bitcast(F32).rearrange("p c d -> p (c d)"),
                                                      ALU.mult, ALU.subtract))
            dve.wait_ge(consts, 1)
            settle(nc.vector.tensor_copy(ident_b[:], ident[:]))
            for u in UR:
                settle(nc.vector.memset(kblk[u][:], 0.0))
            nc.vector.memset(minus_half[:], -0.5).then_inc(wmade, 1)

            for now, order in passes(dve, "vector"):
                def link(ins):
                    ins.then_inc(own.sem[u], 1)
                    dve.wait_ge(own.sem[u], own.next(it, u))

                def statistics(u, src):
                    for g in range(G):
                        a = nc.vector.bn_stats(stats[u][:, g, :], src[g])
                    link(a)
                    nc.vector.memset(var[u][:], 0.0)
                    for g in range(G):
                        a = nc.vector.bn_aggr(mv[u][:, g, :], stats[u][:, g, :])
                    link(a)
                    nc.vector.tensor_scalar(var[u][:], mv[u][:, :, 1], LN_EPS, None, ALU.add)\
                        .then_inc(var_ready[u], 1)

                def normalise(u, src, L):
                    dve.wait_ge(rstd_ready[u], rstd_ready.at(it, L))
                    for g in range(G):
                        a = nc.vector.tensor_scalar(y[u][:, g, :], src[g], mv[u][:, g, 0:1], rstd[u][:, g:g + 1],
                                                    ALU.subtract, ALU.mult)
                    a.then_inc(nrm_ready[u], 1)

                for step, part, u, lag in order:
                    it, b = now - lag, ps[u]
                    if step == "in":
                        own.start(u)
                        dve.wait_ge(x0_hi[u], x0_hi.at(it, 1))
                        nc.vector.tensor_tensor(flat(xT_lo[u]), xt_in[u][:].rearrange("p c g n -> p (c g n)"),
                                                flat(xT_hi[u]).bitcast(F32), ALU.subtract).then_inc(xt_ready[u], 1)
                    if step in ("kv0", "kv2"):
                        a = int(step[-1]) // 2
                        dve.wait_ge(k_ready[u], k_ready.at(it, a + 1))
                        for h in range(HC):
                            q = slice(h * HD, (h + 1) * HD)
                            cp = nc.vector.tensor_copy(kblk[u][q, :, :, h, :],
                                                       kT[u][q].rearrange("p c (g n) -> p c g n", g=G))
                        cp.then_inc(kblk_ready[u], 1)
                    if step[:5] == "score" or step in ("exp0", "exp1", "exp2"):
                        L = int(step[-1])
                        k0 = (0, 4, 5)[L]
                        scale = (1.0, 1.0, float(HD) ** -0.5)[L]
                        ks = [part]

                        def views(k, L=L, u=u, b=b):
                            g, c = divmod(k, NC)
                            if L == 1:
                                return (b[2][:, 0:GN].rearrange("p (g n) -> p g n", g=G), absent[u][:],
                                        rmax[u][:, :, 0, 0], nmax[u][:, :, 0, 0], esum[u][:, :, 0, 0],
                                        rsum[u][:, :, 0, 0], G)
                            return (b[k][:, :].rearrange("p (h n) -> p h n", h=HC),
                                    absent[u][:, g:g + 1, :].to_broadcast([P, HC, P]),
                                    rmax[u][:, g, c], nmax[u][:, g, c], esum[u][:, g, c], rsum[u][:, g, c], HC)

                    if step[:5] == "score":
                        if L == 0 and part == 0:
                            dve.wait_ge(adj_ready[u], adj_ready.at(it, 1))
                        for k in ks:
                            s, m, mx, nm, _, _, n = views(k)
                            dve.wait_ge(s_ready[u], s_ready.at(it, k0 + k + 1))
                            if L == 0:
                                nc.vector.memset(mx, 0.0)
                                link(nc.vector.copy_predicated(s, m, fill[:].unsqueeze(2).to_broadcast([P, n, P])))
                            link(nc.vector.tensor_reduce(mx, s, AX_X, ALU.max))
                            nc.vector.tensor_scalar(nm, mx, -2.0 if L == 2 else -1.0, scale / 2 if L == 2 else 1.0,
                                                    ALU.mult, ALU.mult).then_inc(max_ready[u], 1)
                    if step in ("exp0", "exp1", "exp2"):
                        for k in ks:
                            _, _, _, _, es, rs, _ = views(k)
                            dve.wait_ge(exp_ready[u], exp_ready.at(it, k0 + k + 1))
                            nc.vector.reciprocal(rs, es).then_inc(r_ready[u], 1)
                    if step[:3] == "hop":
                        t = int(step[3])
                        for g in [part]:
                            dve.wait_ge(o_t[u], o_t.at(it, G * t + g + 1))
                            o = b[g][:, 0:D].rearrange("p (c n) -> p c n", c=NC)
                            z = zT[u][:, :, g * P:(g + 1) * P]
                            if t < HOPS:
                                a = nc.vector.scalar_tensor_tensor(z, vT[u][:, :, g * P:(g + 1) * P], ALPHA, o,
                                                                   ALU.mult, ALU.add)
                            else:
                                a = nc.vector.tensor_copy(z, o)
                            a.then_inc(zt_ready[u], 1)
                    if step in ("back3", "back4"):
                            t = int(step[4])
                            if t == HOPS and part == 0:
                                dve.wait_ge(xn_ready[u], xn_ready.at(it, 2))
                            for g in [part]:
                                dve.wait_ge(back[u], back.at(it, (G * t if t < HOPS else G * t + 1) + g + 1))
                                res = x_in[u] if t < HOPS else xnat[u]
                                a = nc.vector.tensor_tensor(y[u][:, g, :], b[2 + g][:, 0:D], res[:, g, :], ALU.add)
                            if part == G - 1:
                                link(a)
                            if t == HOPS and part == G - 1:
                                link(nc.vector.tensor_tensor(y[u][:], y[u][:], rowc("bo2"), ALU.add))
                    if step == "y1":
                        dve.wait_ge(xn_ready[u], xn_ready.at(it, 1))
                        dve.wait_ge(back[u], back.at(it, 9))
                        link(nc.vector.tensor_tensor(flat(y[u]), b[0][:, :], flat(xnat[u]), ALU.add))
                        link(nc.vector.tensor_tensor(y[u][:], y[u][:], rowc("bo1"), ALU.add))
                    if step in ("stat1", "stat2", "stat3"):
                        statistics(u, [y[u][:, g, :] for g in range(G)])
                    if step in ("nrm1", "nrm2", "nrm3"):
                        normalise(u, [y[u][:, g, :] for g in range(G)], int(step[-1]))
                    if step[:5] == "split":
                        dve.wait_ge(xt32[u], xt32.at(it, int(step[-1])))
                        link(nc.vector.tensor_copy(flat(xT_hi[u]), flat(xT[u])))
                        nc.vector.tensor_tensor(flat(xT_lo[u]), flat(xT[u]), flat(xT_hi[u]).bitcast(F32),
                                                ALU.subtract).then_inc(xt_ready[u], 1)
                    if step == "mask":
                        for d in range(LABELS):
                            a = nc.vector.tensor_scalar(E[u][:, :, 0, d], adj_f[u][:], float(d + 1), None,
                                                        ALU.is_equal)
                        link(a)
                        for g in range(G):
                            a = nc.vector.tensor_reduce(cnt[u][:, g], E[u][:, g, 0], AX_X, ALU.add)
                        link(a)
                        link(nc.vector.tensor_scalar(cnt[u][:], cnt[u][:], DEG_EPS, None, ALU.add))
                        nc.vector.reciprocal(rcnt[u][:], cnt[u][:]).then_inc(wm_cnt[u], 1)
                    if step == "agg":
                        for k in [part]:
                            g, c = divmod(k, NC)
                            dve.wait_ge(agg_hi_ready[u], agg_hi_ready.at(it, k + 1))
                            nc.vector.tensor_tensor(agg_lo[u][:, c, :, g, :],
                                                    b[k][:, :].rearrange("p (d n) -> p d n", d=LABELS),
                                                    agg_hi[u][:, c, :, g, :].bitcast(F32),
                                                    ALU.subtract).then_inc(agg_lo_ready[u], 1)
                    if step == "osplit":
                        dve.wait_ge(out32[u], out32.at(it, 1))
                        link(nc.vector.tensor_copy(flat(oT_hi[u]), flat(qT[u])))
                        nc.vector.tensor_tensor(flat(oT_lo[u]), flat(qT[u]), flat(oT_hi[u]).bitcast(F32),
                                                ALU.subtract).then_inc(out_ready[u], 1)
                    if step == "gate" and part == 0:
                        dve.wait_ge(gate_ready[u], gate_ready.at(it, 1))
                        link(nc.vector.tensor_scalar(rT[u][:], rT[u][:], 0.5, 0.5, ALU.mult, ALU.add))
                        for c in range(NC):
                            a = nc.vector.scalar_tensor_tensor(vnat[u][:, c, :], b[3][:, c * GN:(c + 1) * GN],
                                                               colc("bnh", c), rT[u][:, c, :], ALU.add, ALU.mult)
                        link(a)
                    if step == "gate" and part == 1:
                        dve.wait_ge(gates[u], gates.at(it, 3))
                        nc.vector.tensor_tensor(flat(vnat[u]), b[0][:, :], flat(vnat[u]), ALU.add)\
                            .then_inc(r_used[u], 1)
                    if step == "mix" and part == 0:
                        dve.wait_ge(gate_ready[u], gate_ready.at(it, 2))
                        link(nc.vector.tensor_scalar(vT[u][:], vT[u][:], 0.5, 0.5, ALU.mult, ALU.add))
                    if step == "mix" and part == 1:
                        dve.wait_ge(gate_ready[u], gate_ready.at(it, 3))
                        link(nc.vector.tensor_tensor(flat(qT[u]), flat(xT[u]), flat(vnat[u]), ALU.subtract))
                        link(nc.vector.tensor_tensor(flat(qT[u]), flat(qT[u]), flat(vT[u]), ALU.mult))
                        nc.vector.tensor_tensor(flat(qT[u]), flat(qT[u]), flat(vnat[u]), ALU.add)\
                            .then_inc(mixed[u], 1)
                    if step == "stat4":
                        dve.wait_ge(mixed_t[u], mixed_t.at(it, 1))
                        statistics(u, [b[1][:, g * D:(g + 1) * D] for g in range(G)])
                    if step == "last":
                        normalise(u, [b[1][:, g * D:(g + 1) * D] for g in range(G)], 4)
            assert own.used == [DVE_OWN] * UNITS, own.used


_OUTS = [((GRAPHS, P, D), "float32")]


def kernel(**inputs):
    import concourse.bacc as _bacc
    from concourse.bass_utils import run_bass_kernel_spmd as _run

    def chunked(w):
        return np.asarray(w).reshape(-1, P, D).transpose(1, 0, 2)

    v = {k: np.asarray(a) for k, a in inputs.items()}
    w = [v[f"L0_gnn_W{n}"].T for n in "qkv"] + [v[f"L2_gnn_W{n}"] for n in "qkv"]
    w += [v["L3_gnn_Wd"].T[D * d:D * d + D] for d in range(LABELS)]
    w += [v[f"L3_gnn_W{n}"].T for n in ("ri", "zi", "ni", "rh", "zh", "nh")]
    l1 = [v["L1_gnn_Wq"].T, v["L1_gnn_Wk"].T, v["L1_gnn_Wv"].T, v["L1_gnn_Wo"]]
    vec = {f"b{n}{L}": v[f"L{L}_gnn_b{n}"] for L in (0, 2) for n in "qkv"}
    vec.update({f"b{n}": v[f"L3_gnn_b{n}"] for n in ("d", "ri", "rh", "zi", "zh", "ni", "nh")})
    vec.update({f"{n}{L}": v[f"L{L}_gnn_{n}"] for L in range(4) for n in ("gamma", "beta")})
    vec.update({f"bo{L}": v[f"L{L}_gnn_bo"] for L in (1, 2)})
    arrays = {
        "x": v["x"],
        "xt": v["x"].transpose(0, 2, 1),
        "adj": v["adj"],
        "weights": np.stack([chunked(a) for a in w], axis=1),
        "l1_weights": np.stack([chunked(a) for a in l1], axis=1),
        "wo2": chunked(v["L2_gnn_Wo"]),
        "cols": np.stack([vec[n].reshape(NC, P) for n in COLS]).reshape(-1, P).T,
        "rows": np.stack([vec[n] for n in ROWS]),
    }
    arrays = {f"in_{k}": np.ascontiguousarray(a) for k, a in arrays.items()}
    nc = _bacc.Bacc("TRN2", target_bir_lowering=False, num_devices=1)
    args = [nc.dram_tensor(n, a.shape, mybir.dt.from_np(a.dtype), kind="ExternalInput").ap()
            for n, a in arrays.items()]
    args += [nc.dram_tensor(f"out_{i}", shape, mybir.dt.from_np(np.dtype(dt)), kind="ExternalOutput").ap()
             for i, (shape, dt) in enumerate(_OUTS)]
    gnn_program(nc, *args)
    r = _run(nc, [arrays], core_ids=[0])
    return r.results[0]["out_0"]
```

```python
from contextlib import ExitStack

import numpy as np
import concourse.bass as bass
from concourse import mybir

P = 128
GRAPHS = 64
D = 256
NC = D // P
HEADS = 8
HD = D // HEADS
HC = P // HD
LABELS = 4
G = 2
UNITS = 2
ROUNDS = GRAPHS // (G * UNITS)
GN = G * P
LN_EPS = 1e-5
DEG_EPS = 1e-8
ALPHA = 0.1
HOPS = 4

ALU = mybir.AluOpType
ACT = mybir.ActivationFunctionType
AX_X = mybir.AxisListType.X
F32 = mybir.dt.float32
F32R = mybir.dt.float32r
I32 = mybir.dt.int32
BF16 = mybir.dt.bfloat16

SLOTS = ["q0", "k0", "v0", "q2", "k2", "v2", "d0", "d1", "d2", "d3",
         "ri", "zi", "ni", "rh", "zh", "nh"]
LOADED = len(SLOTS)
SLOT = {n: i for i, n in enumerate(SLOTS + ["g1", "vo1"])}
COLS = ["bq0", "bk0", "bv0", "bq2", "bk2", "bd", "bri", "brh", "bzi", "bzh", "bni", "bnh",
        "gamma0", "beta0", "gamma1", "beta1", "gamma2", "beta2"]
COL = {n: NC * i for i, n in enumerate(COLS)}
ROWS = ["gamma0", "beta0", "gamma1", "beta1", "gamma3", "beta3", "bo1", "bo2", "bv2"]
ROW = {n: i for i, n in enumerate(ROWS)}


def by(n, *steps):
    return [(s, p) for s in steps for p in range(n)]


SB = G * NC
HOP_STEPS = [s for t in range(HOPS) for s in (f"hop{t}", f"back{t}")]
PIECES = {
    "tensor": by(4, "qkv0") + by(1, "kv0") + by(SB, "score0", "pt0") + by(G, *HOP_STEPS)
    + by(1, "nrm1") + by(3, "proj1") + by(1, "score1", "pt1", "y1", "nrm2")
    + by(4, "qkv2") + by(SB, "score2", "pt2") + by(G, "hop4", "back4") + by(1, "nrm3")
    + by(G, "wt") + by(SB, "label") + by(1, "out") + by(2, "hidden") + by(3, "gate") + by(1, "mixt"),
    "scalar": by(3, "qkv0") + by(1, "kv0") + [("exp0", 0), ("exp0", 1), ("exp0", 2), ("pt0", 0), ("exp0", 3)]
    + [("pt0", 1), ("pt0", 2), ("pt0", 3)] + by(G, "back0", "back1", "back2")
    + by(1, "nrm1") + by(2, "proj1") + by(1, "exp1", "pt1", "nrm2")
    + by(2, "qkv2") + by(SB, "exp2", "pt2") + by(1, "nrm3")
    + by(G, "wt") + by(SB, "label") + by(1, "out") + [("gate", 0), ("mix", 0), ("gate", 1), ("in+", 0)],
    "gpsimd": by(1, "in") + by(SB, "exp0") + by(1, "stat1", "nrm1", "exp1", "stat2", "nrm2") + by(SB, "exp2")
    + by(1, "stat3", "mask", "stat4", "last"),
    "vector": [("kv0", 0), ("score0", 0), ("score0", 1), ("exp0", 0), ("score0", 2), ("exp0", 1), ("score0", 3)]
    + [("exp0", 2), ("exp0", 3)] + by(G, "hop0", "hop1", "hop2", "hop3", "back3") + by(1, "stat1", "nrm1", "split1")
    + by(1, "score1", "exp1", "y1", "stat2", "nrm2", "split2", "kv2", "qkv2")
    + [("score2", 0), ("score2", 1), ("exp2", 0), ("score2", 2), ("exp2", 1), ("score2", 3), ("exp2", 2), ("exp2", 3)]
    + by(G, "hop4", "back4") + by(1, "stat3", "mask", "nrm3", "split3")
    + by(1, "osplit") + by(2, "gate", "mix") + by(1, "in+", "stat4", "last"),
    "sync": by(1, "nrm1", "last"),
}

TURNS = {
    "tensor": (58, [0, 1, 4, 1, 5, 1, 1, 1, 1, 2, 2, 2, 6, 1, 1, 1, 2, 1, 5, 1, 2, 3, 1, 3, 2, 1, 2, 4, 1, 2,
                   1, 12, 1, 1, 3, 1, 1, 1, 1, 1, 3, 2, 3, 2, 4, 1, 1, 4, 1, 4, 4, 3, 1, 1, 1, 4, 4, 1, 2, 4, 1]),
    "scalar": (37, [0, 3, 4, 1, 3, 1, 3, 1, 2, 3, 4, 1, 2, 3, 1, 2, 1, 5, 2, 1, 1, 6, 2, 1, 1, 1, 3, 2, 1, 1,
                   4, 3, 1, 4, 4, 4, 4, 1, 2, 2, 1]),
    "gpsimd": (16, [5, 3, 2, 4, 3, 2, 3, 1, 1, 2, 2, 6, 2]),
    "vector": (46, [7, 1, 2, 3, 2, 1, 1, 2, 1, 1, 2, 1, 6, 2, 1, 5, 1, 1, 1, 2, 1, 2, 1, 2, 1, 5, 1, 1, 2, 1,
                   6, 1, 1, 1, 1, 2, 1, 1, 4, 1, 2, 4, 1, 12, 1, 1, 2, 1, 5]),
    "sync": (1, [0, 1, 1, 1, 1]),
}


def merged(engine):
    pieces = PIECES[engine]
    at, runs = TURNS[engine]
    order, i, j = [], 0, at
    for k, n in enumerate(runs):
        for _ in range(n):
            if k % 2 == 0:
                order.append((*pieces[i], 0, 0))
                i += 1
            else:
                order.append((*pieces[j % len(pieces)], 1, int(j < len(pieces))))
                j += 1
    assert i == j - at == len(pieces), (engine, i, j)
    return order


def passes(eng, engine):
    order = [(s.rstrip("+"), p, u, behind - s.endswith("+")) for s, p, u, behind in merged(engine)]
    yield -1, [x for x in order if x[-1] == -1]
    yield 0, [x for x in order if x[-1] <= 0]
    with eng.Fori(1, ROUNDS - 1) as n:
        yield n, order
    yield ROUNDS - 1, [x for x in order if x[-1] >= 0]
    yield ROUNDS, [x for x in order if x[-1] == 1]


class Signal:

    def __init__(self, sems, per_round):
        self.sem, self.per_round = sems, per_round

    def __getitem__(self, u):
        return self.sem[u]

    def at(self, it, k):
        return it * self.per_round + k


class Own:

    def __init__(self, sems, per_round):
        self.sem, self.per_round, self.used = sems, per_round, [0] * len(sems)

    def next(self, it, u):
        self.used[u] = self.used[u] % self.per_round + 1
        return it * self.per_round + self.used[u]


DVE_OWN = 32
POOL_OWN = 3


def gnn_program(nc, x, xt, adj, weights, l1_weights, wo2, cols, rows, out):
    ctx = ExitStack()
    with ctx:
        def sb(name, shape, dt=F32):
            return ctx.enter_context(nc.sbuf_tensor(name, shape, dt))

        def sem(name):
            return ctx.enter_context(nc.semaphore(name))

        def per_unit(name, shape, dt=F32):
            return [sb(f"{name}_{u}", shape, dt) for u in range(UNITS)]

        def aliased(name, over, shape, dt):
            return [nc.alloc_sbuf_tensor_at(f"{name}_{u}", shape, dt, offset=nc.lookup_mloc(over[u]).addr) for u in range(UNITS)]

        ident = sb("ident", [P, P])
        ident_b = sb("ident_b", [P, P], BF16)
        w_hi = sb("w_hi", [P, len(SLOT), NC, D], F32R)
        w_lo = sb("w_lo", [P, len(SLOT), NC, D], F32R)
        wo2_sb = sb("wo2_sb", [P, NC, D])
        col = sb("col", [P, NC * len(COLS)])
        half = sb("half", [P, 2 * NC])
        row = sb("row", [P, len(ROWS), D])
        fill = sb("fill", [P, 1])
        minus_half = sb("minus_half", [P, G])
        pidle = sb("pidle", [P, 1])
        psink = [sb(f"psink_{u}", [P, 1]) for u in range(2)]

        x_in = per_unit("x_in", [P, G, D])
        xt_in = per_unit("xt_in", [P, NC, G, P])
        adj_in = per_unit("adj_in", [P, G, P], I32)
        absent = per_unit("absent", [P, G, P], I32)
        no_edge = per_unit("no_edge", [P, G, P], BF16)
        adj_f = per_unit("adj_f", [P, G, P])
        xT = per_unit("xT", [P, NC, GN])
        xT_hi = per_unit("xT_hi", [P, NC, GN], F32R)
        xT_lo = per_unit("xT_lo", [P, NC, GN], F32R)
        xnat = per_unit("xnat", [P, G, D])
        y = per_unit("y", [P, G, D])
        qT = per_unit("qT", [P, NC, GN])
        kT = per_unit("kT", [P, NC, GN])
        vT = per_unit("vT", [P, NC, GN])
        vnat = per_unit("vnat", [P, G, D])
        kblk = per_unit("kblk", [P, NC, G, HC, P])
        E = per_unit("E", [P, G, NC, HC, P])
        PT = per_unit("PT", [P, G, NC, HC, P])
        wT = per_unit("wT", [P, G, LABELS, P])
        oT_hi = per_unit("oT_hi", [P, NC, GN], F32R)
        oT_lo = per_unit("oT_lo", [P, NC, GN], F32R)
        nmax = per_unit("nmax", [P, G, NC, HC])
        rmax = per_unit("rmax", [P, G, NC, HC])
        esum = per_unit("esum", [P, G, NC, HC])
        rsum = per_unit("rsum", [P, G, NC, HC])
        cnt = per_unit("cnt", [P, G, LABELS])
        rcnt = per_unit("rcnt", [P, G, LABELS])
        stats = per_unit("stats", [P, G, 6])
        mv = per_unit("mv", [P, G, 2])
        var = per_unit("var", [P, G])
        rstd = per_unit("rstd", [P, G])
        zT, rT = kT, kT
        xw = aliased("xw", PT, [P, G, LABELS, D], F32)

        ps = [[ctx.enter_context(nc.psum_tensor(f"bank_{u}_{b}", [P, 512], F32)) for b in range(4)]
              for u in range(UNITS)]

        def signal(name, per_round):
            return Signal([sem(f"{name}_{u}") for u in range(UNITS)], per_round)

        loaded = signal("loaded", 4 * 16)
        adj_ready = signal("adj_ready", 2)
        x0_hi = signal("x0_hi", 1)
        xt32 = signal("xt32", 3)
        xt_ready = signal("xt_ready", 4)
        proj = signal("proj", 8)
        q_ready = signal("q_ready", 3)
        v2_ready = signal("v2_ready", 1)
        xhi_ready = signal("xhi_ready", 3)
        k_ready = signal("k_ready", 2)
        kblk_ready = signal("kblk_ready", 2)
        v_ready = signal("v_ready", 1)
        vback = signal("vback", 1)
        vn_ready = signal("vn_ready", 2)
        s_ready = signal("s_ready", 9)
        max_ready = signal("max_ready", 9)
        exp_ready = signal("exp_ready", 9)
        r_ready = signal("r_ready", 9)
        e_ready = signal("e_ready", 9)
        p_t = signal("p_t", 9)
        pt_ready = signal("pt_ready", 9)
        o_t = signal("o_t", 10)
        zt_ready = signal("zt_ready", 10)
        back = signal("back", 11)
        z_ready = signal("z_ready", 6)
        var_ready = signal("var_ready", 4)
        rstd_ready = signal("rstd_ready", 4)
        nrm_ready = signal("nrm_ready", 4)
        n_t = signal("n_t", 3)
        xn_ready = signal("xn_ready", 3)
        bank1_free = signal("bank1_free", 1)
        wm_cnt = signal("wm_cnt", 1)
        wm_ready = signal("wm_ready", 1)
        w_t = signal("w_t", 2)
        wt_ready = signal("wt_ready", 2)
        labelled = signal("labelled", 4)
        xw_ready = signal("xw_ready", 4)
        out_t = signal("out_t", 1)
        out32 = signal("out32", 1)
        out_ready = signal("out_ready", 1)
        gates = signal("gates", 3)
        gate_ready = signal("gate_ready", 3)
        r_used = signal("r_used", 1)
        mixed = signal("mixed", 1)
        mixed_t = signal("mixed_t", 1)
        stored = signal("stored", 16)

        w_loaded = [sem(f"w_loaded_{j}") for j in range(LOADED // 4 + 1)]
        c_loaded, w_split, w_read, l1_prod, consts = (
            sem(n) for n in ("c_loaded", "w_split", "w_read", "l1_prod", "consts"))
        wmade = sem("wmade")
        dve_own = Own([sem(f"dve_own_{u}") for u in range(UNITS)], DVE_OWN)
        pool_own = Own([sem(f"pool_own_{u}") for u in range(UNITS)], POOL_OWN)
        dve_pre, pool_pre = sem("dve_pre"), sem("pool_pre")

        UR = range(UNITS)
        x_v = x.rearrange("(r u g) n d -> r u n g d", u=UNITS, g=G)
        xt_v = xt.rearrange("(r u g) (c p) n -> r u p c g n", u=UNITS, g=G, p=P)
        adj_v = adj.rearrange("(r u g) n m -> r u n g m", u=UNITS, g=G)
        out_v = out.rearrange("(r u g) n d -> r u n g d", u=UNITS, g=G)

        def rowc(name, n=G):
            return row[:, ROW[name]:ROW[name] + 1, :].to_broadcast([P, n, D])

        def colc(name, c):
            return col[:, COL[name] + c:COL[name] + c + 1]

        def flat(t):
            return t[:].rearrange("p a b -> p (a b)")

        stage = [kblk[j][:].rearrange("p c g h n -> p (c g h n)").rearrange("p (s c d) -> p s c d", s=4, c=NC)
                 for j in UR]
        WR = LOADED // 4
        block = ctx.enter_context(nc.Block())

        @block.sync
        def _(sp):
            sp.dma_start(col[:], cols).then_inc(c_loaded, 16)
            sp.dma_start(row[:], rows.unsqueeze(0).to_broadcast([P, len(ROWS), D])).then_inc(c_loaded, 16)
            sp.dma_start(wo2_sb[:], wo2).then_inc(c_loaded, 16)
            for j in range(WR):
                if j >= 2:
                    sp.wait_ge(w_split, j - 1)
                sp.dma_start(stage[j % 2], weights[:, 4 * j:4 * j + 4]).then_inc(w_loaded[j], 16)
            sp.wait_ge(w_split, WR - 1)
            sp.dma_start(stage[WR % 2], l1_weights).then_inc(w_loaded[WR], 16)

            def load(r, u):
                sp.dma_start(x_in[u][:], x_v[r, u]).then_inc(loaded[u], 16)
                for c in range(NC):
                    sp.dma_start(xt_in[u][:, c], xt_v[r, u][:, c]).then_inc(loaded[u], 16)
                sp.dma_start(adj_in[u][:], adj_v[r, u]).then_inc(loaded[u], 16)

            def store(r, u, it):
                sp.wait_ge(xn_ready[u], xn_ready.at(it, 3))
                sp.dma_start(out_v[r, u], xnat[u][:]).then_inc(stored[u], 16)

            for u in UR:
                load(0, u)

            def moves(now, order):
                for step, _, u, lag in order:
                    it = now - lag
                    if step == "nrm1" and not (isinstance(it, int) and it + 1 >= ROUNDS):
                        sp.wait_ge(adj_ready[u], adj_ready.at(it, 2))
                        sp.wait_ge(nrm_ready[u], nrm_ready.at(it, 1))
                        load(it + 1, u)
                    if step == "last":
                        store(it, u, it)

            for now, order in passes(sp, "sync"):
                moves(now, order)
            for u in UR:
                sp.wait_ge(stored[u], stored.at(ROUNDS, 16))

        @block.tensor
        def _(pe):
            def accumulate(groups, hi, lo, first, last):
                whole = first and last
                for k, (o, terms) in enumerate(groups):
                    chosen = [t for t, low in terms if (lo if low else hi)]
                    for i, (a, w) in enumerate(chosen):
                        mm = nc.tensor.matmul(o, a, w, start=first and i == 0 and (whole or k == 0),
                                              stop=last and i == len(chosen) - 1 and (whole or k == len(groups) - 1))
                return mm

            def project(bank, names, hi=True, lo=True, first=None, last=None):
                def terms(oc):
                    for n, xh, xl in names:
                        w = slice(oc * P, (oc + 1) * P)
                        for kc in range(NC):
                            yield (w_hi[:, SLOT[n], kc, w], xh(kc)), False
                            yield (w_lo[:, SLOT[n], kc, w], xh(kc)), False
                        for kc in range(NC):
                            yield (w_hi[:, SLOT[n], kc, w], xl(kc)), True
                return accumulate([(bank[:, oc * GN:(oc + 1) * GN], list(terms(oc))) for oc in range(NC)],
                                  hi, lo, hi if first is None else first, lo if last is None else last)

            def natural(bank, n, u, hi=True, lo=True):
                def terms(g):
                    xs = slice(g * P, (g + 1) * P)
                    for c in range(NC):
                        yield (xT_hi[u][:, c, xs], w_hi[:, SLOT[n], c, :]), False
                        yield (xT_hi[u][:, c, xs], w_lo[:, SLOT[n], c, :]), False
                    for c in range(NC):
                        yield (xT_lo[u][:, c, xs], w_hi[:, SLOT[n], c, :]), True
                return accumulate([(bank[:, g * D:(g + 1) * D], list(terms(g))) for g in range(G)], hi, lo, hi, lo)

            pe.wait_ge(w_loaded[WR], 16)
            s = stage[WR % 2]
            for b, (i, j) in enumerate(((0, 1), (2, 3))):
                for kc in range(NC):
                    for jc in range(NC):
                        mm = nc.tensor.matmul(ps[0][b][:, kc * D:(kc + 1) * D], s[:, i, jc, kc * P:(kc + 1) * P],
                                              s[:, j, jc, :], start=jc == 0, stop=jc == NC - 1)
                mm.then_inc(l1_prod, 1)
            pe.wait_ge(wmade, 1)

            for now, order in passes(pe, "tensor"):
                def x_parts(u):
                    return (lambda kc: xT_hi[u][:, kc, :], lambda kc: xT_lo[u][:, kc, :])

                for step, part, u, lag in order:
                    it, b = now - lag, ps[u]
                    if step in ("qkv0", "qkv2"):
                        L = int(step[-1])
                        names = [[(f"{n}{L}", *x_parts(u))] for n in "kq"]
                        if part == 0:
                            if L == 0:
                                pe.wait_ge(x0_hi[u], x0_hi.at(it, 1))
                            else:
                                pe.wait_ge(xhi_ready[u], xhi_ready.at(it, L))
                            project(b[2], names[0], lo=False)
                            project(b[0], names[1], lo=False)
                        if part == 1:
                            pe.wait_ge(xt_ready[u], xt_ready.at(it, L + 1))
                            project(b[2], names[0], hi=False).then_inc(proj[u], 1)
                        if part == 2:
                            project(b[0], names[1], hi=False).then_inc(proj[u], 1)
                        if part == 3 and L == 0:
                            pe.wait_ge(bank1_free[u], bank1_free.at(it, 1))
                            project(b[1], [("v0", *x_parts(u))]).then_inc(proj[u], 1)
                        if part == 3 and L == 2:
                            natural(b[1], "v2", u).then_inc(proj[u], 1)
                    if step == "kv0":
                        pe.wait_ge(v_ready[u], v_ready.at(it, 1))
                        for g in range(G):
                            for c in range(NC):
                                mm = nc.tensor.transpose(b[3][:, (g * NC + c) * P:(g * NC + c + 1) * P],
                                                         vT[u][:, c, g * P:(g + 1) * P], ident[:])
                        mm.then_inc(vback[u], 1)
                    if step in ("score0", "score2"):
                        L = int(step[-1])
                        a = L // 2
                        k = part
                        g, c = divmod(k, NC)
                        if k == 0:
                            pe.wait_ge(q_ready[u], q_ready.at(it, L + 1))
                            pe.wait_ge(kblk_ready[u], kblk_ready.at(it, a + 1))
                        if L == 0 and k == 3:
                            pe.wait_ge(vn_ready[u], vn_ready.at(it, 1))
                        if L == 2 and k == 1:
                            pe.wait_ge(v2_ready[u], v2_ready.at(it, 1))
                        mm = nc.tensor.matmul(b[k][:, :], qT[u][:, c, g * P:(g + 1) * P],
                                              kblk[u][:, c, g].rearrange("p h n -> p (h n)"),
                                              start=True, stop=L == 0)
                        if L == 2:
                            mm = nc.tensor.matmul(b[k][:, :], ident_b[:],
                                                  no_edge[u][:, g:g + 1, :].to_broadcast([P, HC, P]),
                                                  start=False, stop=True)
                        mm.then_inc(s_ready[u], 1)
                    if step in ("pt0", "pt2"):
                        k0 = 0 if step == "pt0" else 5
                        k = part
                        g, c = divmod(k, NC)
                        pe.wait_ge(e_ready[u], e_ready.at(it, k0 + k + 1))
                        for h in range(HC):
                            mm = nc.tensor.transpose(b[k][:, h * P:(h + 1) * P], E[u][:, g, c, h], ident[:])
                        mm.then_inc(p_t[u], 1)
                    if step[:3] == "hop":
                        t = int(step[3])
                        if t in (0, HOPS) and part == 0:
                            pe.wait_ge(pt_ready[u], pt_ready.at(it, 4 if t == 0 else 9))
                        for g in [part]:
                            if 0 < t < HOPS:
                                pe.wait_ge(z_ready[u], z_ready.at(it, G * (t - 1) + g + 1))
                            for h in range(HEADS):
                                c, hh = divmod(h, HC)
                                mm = nc.tensor.matmul(b[g][hh * HD:(hh + 1) * HD, c * P:(c + 1) * P],
                                                      vnat[u][:, g, h * HD:(h + 1) * HD], PT[u][:, g, c, hh],
                                                      start=True, stop=True)
                            mm.then_inc(o_t[u], 1)
                    if step[:4] == "back":
                        t = int(step[4])
                        for g in [part]:
                            pe.wait_ge(zt_ready[u], zt_ready.at(it, G * t + g + 1))
                            for c in range(NC):
                                zc = zT[u][:, c, g * P:(g + 1) * P]
                                if t < HOPS:
                                    mm = nc.tensor.transpose(b[2 + g][:, c * P:(c + 1) * P], zc, ident[:])
                                else:
                                    mm = nc.tensor.matmul(b[2 + g][:, 0:D], zc, wo2_sb[:, c, :],
                                                          start=c == 0, stop=c == NC - 1)
                            mm.then_inc(back[u], 1)
                    if step in ("nrm1", "nrm2", "nrm3"):
                        L = int(step[-1])
                        pe.wait_ge(nrm_ready[u], nrm_ready.at(it, L))
                        for c in range(NC):
                            for g in range(G):
                                mm = nc.tensor.transpose(b[3][:, c * GN + g * P:c * GN + (g + 1) * P],
                                                         y[u][:, g, c * P:(c + 1) * P], ident[:])
                        mm.then_inc(n_t[u], 1)
                    if step == "proj1":
                        if part == 0:
                            pe.wait_ge(xhi_ready[u], xhi_ready.at(it, 1))
                            project(b[0], [("g1", *x_parts(u))], lo=False)
                            natural(b[1], "vo1", u, lo=False)
                        if part == 1:
                            pe.wait_ge(xt_ready[u], xt_ready.at(it, 2))
                            project(b[0], [("g1", *x_parts(u))], hi=False).then_inc(proj[u], 1)
                        if part == 2:
                            natural(b[1], "vo1", u, hi=False).then_inc(proj[u], 1)
                    if step == "score1":
                        pe.wait_ge(q_ready[u], q_ready.at(it, 2))
                        for g in range(G):
                            for c in range(NC):
                                xs = slice(g * P, (g + 1) * P)
                                nc.tensor.matmul(b[2][:, g * P:(g + 1) * P], qT[u][:, c, xs], xT[u][:, c, xs],
                                                 start=c == 0, stop=False)
                            mm = nc.tensor.matmul(b[2][:, g * P:(g + 1) * P], ident_b[:], no_edge[u][:, g, :],
                                                  start=False, stop=True)
                        mm.then_inc(s_ready[u], 1)
                    if step == "pt1":
                        pe.wait_ge(e_ready[u], e_ready.at(it, 5))
                        for g in range(G):
                            mm = nc.tensor.transpose(b[3][:, g * P:(g + 1) * P], E[u][:, g, 0, 0], ident[:])
                        mm.then_inc(p_t[u], 1)
                    if step == "y1":
                        pe.wait_ge(pt_ready[u], pt_ready.at(it, 5))
                        pe.wait_ge(vn_ready[u], vn_ready.at(it, 2))
                        for g in range(G):
                            mm = nc.tensor.matmul(b[0][:, g * D:(g + 1) * D], PT[u][:, g, 0, 0], vnat[u][:, g, :],
                                                  start=True, stop=True)
                        mm.then_inc(back[u], 1)
                    if step == "wt":
                        if part == 0:
                            pe.wait_ge(wm_ready[u], wm_ready.at(it, 1))
                            pe.wait_ge(xt_ready[u], xt_ready.at(it, 4))
                        for g in [part]:
                            for d in range(LABELS):
                                mm = nc.tensor.transpose(b[g][:, d * P:(d + 1) * P], E[u][:, g, 0, d], ident[:])
                            mm.then_inc(w_t[u], 1)
                    if step == "label":
                        g, pair = divmod(part, LABELS // 2)
                        if part == G:
                            pe.wait_ge(wt_ready[u], wt_ready.at(it, 2))
                        o = b[(part + 2) % 4][:, :]
                        n = SLOT[f"d{2 * pair}"]
                        for kc in range(NC):
                            for j, (a, w) in enumerate(((xT_hi, w_hi), (xT_lo, w_hi), (xT_hi, w_lo))):
                                mm = nc.tensor.matmul(o, a[u][:, kc, g * P:(g + 1) * P], w[:, n:n + 2, kc, :],
                                                      start=kc == 0 and j == 0, stop=kc == NC - 1 and j == 2)
                        mm.then_inc(labelled[u], 1)
                    if step == "out":
                        pe.wait_ge(xw_ready[u], xw_ready.at(it, 4))
                        for c in range(NC):
                            for g in range(G):
                                for d in range(LABELS):
                                    mm = nc.tensor.matmul(b[2][:, c * GN + g * P:c * GN + (g + 1) * P],
                                                          xw[u][:, g, d, c * P:(c + 1) * P], wT[u][:, g, d],
                                                          start=d == 0, stop=d == LABELS - 1)
                        mm.then_inc(out_t[u], 1)
                    if step == "hidden":
                        if part == 0:
                            project(b[3], [("nh", *x_parts(u))])
                        else:
                            project(b[1], [("rh", *x_parts(u))], last=False)
                    if step == "gate":
                        o_parts = (lambda kc: oT_hi[u][:, kc, :], lambda kc: oT_lo[u][:, kc, :])
                        if part == 0:
                            pe.wait_ge(out_ready[u], out_ready.at(it, 1))
                            mm = project(b[1], [("ri", *o_parts)], first=False)
                        if part == 1:
                            mm = project(b[0], [("ni", *o_parts)])
                        if part == 2:
                            mm = project(b[2], [("zh", *x_parts(u)), ("zi", *o_parts)])
                        mm.then_inc(gates[u], 1)
                    if step == "mixt":
                        pe.wait_ge(mixed[u], mixed.at(it, 1))
                        for g in range(G):
                            for c in range(NC):
                                mm = nc.tensor.transpose(b[1][:, g * D + c * P:g * D + (c + 1) * P],
                                                         qT[u][:, c, g * P:(g + 1) * P], ident[:])
                        mm.then_inc(mixed_t[u], 1)

        @block.scalar
        def _(act):
            for j in range(WR):
                act.wait_ge(w_loaded[j], 16)
                nc.scalar.activation(w_hi[:, 4 * j:4 * j + 4].rearrange("p s c d -> p (s c d)"),
                                     stage[j % 2].rearrange("p s c d -> p (s c d)"), ACT.Copy).then_inc(w_read, 1)
            for b, (n, scale) in enumerate((("g1", float(D) ** -0.5), ("vo1", 1.0))):
                act.wait_ge(l1_prod, b + 1)
                nc.scalar.activation(w_hi[:, SLOT[n]].rearrange("p c d -> p (c d)"), ps[0][b][:, :], ACT.Copy,
                                     scale=scale).then_inc(w_read, 1)
            act.wait_ge(wmade, 1)
            for now, order in passes(act, "scalar"):
                for step, part, u, lag in order:
                    it, b = now - lag, ps[u]
                    if step == "in":
                        act.wait_ge(loaded[u], loaded.at(it, 64))
                        nc.scalar.activation(adj_f[u][:], adj_in[u][:], ACT.Copy)
                        nc.scalar.activation(flat(xT_hi[u]), xt_in[u][:].rearrange("p c g n -> p (c g n)"),
                                             ACT.Copy).then_inc(x0_hi[u], 1)
                    if step in ("qkv0", "qkv2"):
                        L = int(step[-1])
                        p0 = 0 if L == 0 else 5
                        o, n, t, ready = ((2, "k", kT, k_ready), (0, "q", qT, q_ready), (1, "v", vT, v_ready))[part]
                        act.wait_ge(proj[u], proj.at(it, p0 + part + 1))
                        for c in range(NC):
                            a = nc.scalar.activation(t[u][:, c, :], b[o][:, c * GN:(c + 1) * GN], ACT.Identity,
                                                     bias=colc(f"b{n}{L}", c))
                        a.then_inc(ready[u], 1)
                    if step == "kv0":
                        act.wait_ge(vback[u], vback.at(it, 1))
                        nc.scalar.activation(flat(vnat[u]), b[3][:, :], ACT.Copy).then_inc(vn_ready[u], 1)
                    if step in ("exp0", "exp2"):
                        k0 = 0 if step == "exp0" else 5
                        scale = 1.0 if step == "exp0" else float(HD) ** -0.5
                        for k in [part]:
                            g, c = divmod(k, NC)
                            act.wait_ge(max_ready[u], max_ready.at(it, k0 + k + 1))
                            for h in range(HC):
                                a = nc.scalar.activation(E[u][:, g, c, h], b[k][:, h * P:(h + 1) * P], ACT.Exp,
                                                         bias=nmax[u][:, g, c, h:h + 1], scale=scale,
                                                         accum_out=esum[u][:, g, c, h:h + 1])
                            a.then_inc(exp_ready[u], 1)
                    if step in ("pt0", "pt2"):
                        k0 = 0 if step == "pt0" else 5
                        for k in [part]:
                            g, c = divmod(k, NC)
                            act.wait_ge(p_t[u], p_t.at(it, k0 + k + 1))
                            nc.scalar.activation(PT[u][:, g, c].rearrange("p h n -> p (h n)"), b[k][:, :],
                                                 ACT.Copy, scale=1.0 - ALPHA if k0 == 0 else 1.0)\
                                .then_inc(pt_ready[u], 1)
                    if step in ("back0", "back1", "back2"):
                        t = int(step[4])
                        for g in [part]:
                            act.wait_ge(back[u], back.at(it, G * t + g + 1))
                            nc.scalar.activation(vnat[u][:, g, :], b[2 + g][:, 0:D], ACT.Copy).then_inc(z_ready[u], 1)
                    if step in ("nrm1", "nrm2", "nrm3"):
                        L = int(step[-1])
                        act.wait_ge(n_t[u], n_t.at(it, L))
                        for to, ready in ((xT_hi, xhi_ready), (xT, xt32)):
                            for c in range(NC):
                                a = nc.scalar.activation(to[u][:, c, :], b[3][:, c * GN:(c + 1) * GN], ACT.Identity,
                                                         bias=colc(f"beta{L - 1}", c), scale=colc(f"gamma{L - 1}", c))
                            a.then_inc(ready[u], 1)
                    if step == "proj1":
                        to, ready = ((qT, q_ready), (vnat, vn_ready))[part]
                        act.wait_ge(proj[u], proj.at(it, 4 + part))
                        nc.scalar.activation(flat(to[u]), b[part][:, :], ACT.Copy).then_inc(ready[u], 1)
                    if step == "exp1":
                        act.wait_ge(max_ready[u], max_ready.at(it, 5))
                        for g in range(G):
                            a = nc.scalar.activation(E[u][:, g, 0, 0], b[2][:, g * P:(g + 1) * P], ACT.Exp,
                                                     bias=nmax[u][:, g, 0, 0:1], accum_out=esum[u][:, g, 0, 0:1])
                        a.then_inc(exp_ready[u], 1)
                    if step == "pt1":
                        act.wait_ge(p_t[u], p_t.at(it, 5))
                        nc.scalar.activation(PT[u][:, :, 0, 0], b[3][:, 0:GN].rearrange("p (g n) -> p g n", g=G),
                                             ACT.Copy).then_inc(pt_ready[u], 1)
                    if step == "wt":
                        for g in [part]:
                            act.wait_ge(w_t[u], w_t.at(it, g + 1))
                            nc.scalar.activation(wT[u][:, g].rearrange("p d n -> p (d n)"), b[g][:, :],
                                                 ACT.Copy).then_inc(wt_ready[u], 1)
                    if step == "label":
                        g, pair = divmod(part, LABELS // 2)
                        act.wait_ge(labelled[u], labelled.at(it, part + 1))
                        nc.scalar.activation(xw[u][:, g, 2 * pair:2 * pair + 2].rearrange("p d f -> p (d f)"),
                                             b[(part + 2) % 4][:, :], ACT.Copy).then_inc(xw_ready[u], 1)
                    if step == "out":
                        act.wait_ge(out_t[u], out_t.at(it, 1))
                        for c in range(NC):
                            a = nc.scalar.activation(qT[u][:, c, :], b[2][:, c * GN:(c + 1) * GN], ACT.Relu,
                                                     bias=colc("bd", c))
                        a.then_inc(out32[u], 1)
                    if step == "gate":
                        for i, t in ((part, (rT, vT)[part]),):
                            act.wait_ge(gates[u], gates.at(it, 2 * i + 1))
                            for c in range(NC):
                                a = nc.scalar.activation(t[u][:, c, :], b[i + 1][:, c * GN:(c + 1) * GN], ACT.Tanh,
                                                         bias=half[:, NC * i + c:NC * i + c + 1], scale=0.5)
                            a.then_inc(gate_ready[u], 1)
                    if step == "mix":
                        act.wait_ge(r_used[u], r_used.at(it, 1))
                        for c in range(NC):
                            v = vnat[u][:, c, :]
                            a = nc.scalar.activation(v, v, ACT.Tanh, bias=colc("bni", c))
                        a.then_inc(gate_ready[u], 1)

        @block.gpsimd
        def _(pool):
            own = pool_own

            nc.gpsimd.memset(pidle[:], 0.0)
            nc.gpsimd.memset(ident[:], 0.0).then_inc(pool_pre, 1)
            pool.wait_ge(pool_pre, 1)
            nc.gpsimd.affine_select(out=ident[:], in_=ident[:], compare_op=ALU.not_equal, fill=1.0, base=0,
                                    pattern=[[-1, P]], channel_multiplier=1).then_inc(consts, 1)
            for u in UR:
                pool.sem_inc(stored[u], 16)
                pool.sem_inc(bank1_free[u], 1)
            pool.wait_ge(wmade, 1)
            for now, order in passes(pool, "gpsimd"):
                def scale_shift(u, gamma, beta):
                    nc.gpsimd.tensor_tensor(xnat[u][:], y[u][:], rowc(gamma), ALU.mult).then_inc(own.sem[u], 1)
                    pool.wait_ge(own.sem[u], own.next(it, u))
                    return nc.gpsimd.tensor_tensor(xnat[u][:], xnat[u][:], rowc(beta), ALU.add)

                for step, part, u, lag in order:
                    it, b = now - lag, ps[u]
                    if step == "in":
                        pool.wait_ge(loaded[u], loaded.at(it, 64))
                        nc.gpsimd.tensor_tensor(psink[u][:], pidle[:], pidle[:], ALU.mult)
                        nc.gpsimd.tensor_scalar(absent[u][:], adj_in[u][:], 0.0, None, ALU.is_equal)\
                            .then_inc(adj_ready[u], 1)
                        nc.gpsimd.tensor_scalar(no_edge[u][:], adj_in[u][:], 0.0, -3e38, ALU.is_equal, ALU.mult)\
                            .then_inc(adj_ready[u], 1)
                    if step in ("exp0", "exp1", "exp2"):
                        k0 = {"exp0": 0, "exp1": 4, "exp2": 5}[step]
                        for k in [part]:
                            g, c = divmod(k, NC)
                            pool.wait_ge(r_ready[u], r_ready.at(it, k0 + k + 1))
                            if step == "exp1":
                                e, r = E[u][:, :, 0, 0], rsum[u][:, :, 0, 0:1].to_broadcast([P, G, P])
                            else:
                                e, r = E[u][:, g, c], rsum[u][:, g, c].unsqueeze(2).to_broadcast([P, HC, P])
                            nc.gpsimd.tensor_tensor(e, e, r, ALU.mult).then_inc(e_ready[u], 1)
                    if step in ("stat1", "stat2", "stat3", "stat4"):
                        pool.wait_ge(var_ready[u], var_ready.at(it, int(step[-1])))
                        nc.gpsimd.tensor_tensor(rstd[u][:], var[u][:], minus_half[:], ALU.pow)\
                            .then_inc(rstd_ready[u], 1)
                    if step in ("nrm1", "nrm2"):
                        L = int(step[-1])
                        pool.wait_ge(nrm_ready[u], nrm_ready.at(it, L))
                        if L == 1:
                            pool.wait_ge(stored[u], stored.at(it, 16))
                        scale_shift(u, f"gamma{L - 1}", f"beta{L - 1}").then_inc(xn_ready[u], 1)
                    if step == "mask":
                        pool.wait_ge(wm_cnt[u], wm_cnt.at(it, 1))
                        for g in range(G):
                            w = E[u][:, g, 0]
                            a = nc.gpsimd.tensor_tensor(w, w, rcnt[u][:, g].unsqueeze(2).to_broadcast([P, LABELS, P]),
                                                        ALU.mult)
                        a.then_inc(wm_ready[u], 1)
                    if step == "last":
                        pool.wait_ge(nrm_ready[u], nrm_ready.at(it, 4))
                        scale_shift(u, "gamma3", "beta3").then_inc(xn_ready[u], 1)
            assert own.used == [POOL_OWN] * UNITS, own.used

        @block.vector
        def _(dve):
            own = dve_own
            pre = [0]

            def settle(ins):
                pre[0] += 1
                ins.then_inc(dve_pre, 1)
                dve.wait_ge(dve_pre, pre[0])

            nc.vector.memset(fill[:], -16384.0)
            dve.wait_ge(c_loaded, 48)
            for i, n in enumerate("rz"):
                for c in range(NC):
                    settle(nc.vector.tensor_tensor(half[:, NC * i + c:NC * i + c + 1], colc(f"b{n}i", c),
                                                   colc(f"b{n}h", c), ALU.add))
            settle(nc.vector.tensor_scalar(half[:], half[:], 0.5, None, ALU.mult))
            for j in range(WR):
                dve.wait_ge(w_read, j + 1)
                nc.vector.tensor_tensor(w_lo[:, 4 * j:4 * j + 4].rearrange("p s c d -> p (s c d)"),
                                        stage[j % 2].rearrange("p s c d -> p (s c d)"),
                                        w_hi[:, 4 * j:4 * j + 4].bitcast(F32).rearrange("p s c d -> p (s c d)"),
                                        ALU.subtract).then_inc(w_split, 1)
            for b, (n, scale) in enumerate((("g1", float(D) ** -0.5), ("vo1", 1.0))):
                dve.wait_ge(w_read, WR + b + 1)
                settle(nc.vector.scalar_tensor_tensor(w_lo[:, SLOT[n]].rearrange("p c d -> p (c d)"), ps[0][b][:, :],
                                                      scale, w_hi[:, SLOT[n]].bitcast(F32).rearrange("p c d -> p (c d)"),
                                                      ALU.mult, ALU.subtract))
            dve.wait_ge(consts, 1)
            settle(nc.vector.tensor_copy(ident_b[:], ident[:]))
            for beta, bo in (("beta0", "bo1"), ("beta1", "bo2")):
                settle(nc.vector.tensor_tensor(rowc(beta, 1), rowc(beta, 1), rowc(bo, 1), ALU.add))
            for u in UR:
                settle(nc.vector.memset(kblk[u][:], 0.0))
            nc.vector.memset(minus_half[:], -0.5).then_inc(wmade, 1)

            for now, order in passes(dve, "vector"):
                def link(ins):
                    ins.then_inc(own.sem[u], 1)
                    dve.wait_ge(own.sem[u], own.next(it, u))

                def statistics(u, src):
                    for g in range(G):
                        a = nc.vector.bn_stats(stats[u][:, g, :], src[g])
                    link(a)
                    nc.vector.memset(var[u][:], 0.0)
                    for g in range(G):
                        a = nc.vector.bn_aggr(mv[u][:, g, :], stats[u][:, g, :])
                    link(a)
                    nc.vector.tensor_scalar(var[u][:], mv[u][:, :, 1], LN_EPS, None, ALU.add)\
                        .then_inc(var_ready[u], 1)

                def normalise(u, src, L):
                    dve.wait_ge(rstd_ready[u], rstd_ready.at(it, L))
                    for g in range(G):
                        a = nc.vector.tensor_scalar(y[u][:, g, :], src[g], mv[u][:, g, 0:1], rstd[u][:, g:g + 1],
                                                    ALU.subtract, ALU.mult)
                    a.then_inc(nrm_ready[u], 1)

                for step, part, u, lag in order:
                    it, b = now - lag, ps[u]
                    if step == "in":
                        dve.wait_ge(x0_hi[u], x0_hi.at(it, 1))
                        nc.vector.tensor_tensor(flat(xT_lo[u]), xt_in[u][:].rearrange("p c g n -> p (c g n)"),
                                                flat(xT_hi[u]).bitcast(F32), ALU.subtract).then_inc(xt_ready[u], 1)
                    if step == "qkv2":
                        dve.wait_ge(proj[u], proj.at(it, 8))
                        nc.vector.tensor_tensor(vnat[u][:], b[1][:, :].rearrange("p (g f) -> p g f", g=G),
                                                rowc("bv2"), ALU.add).then_inc(v2_ready[u], 1)
                    if step in ("kv0", "kv2"):
                        a = int(step[-1]) // 2
                        dve.wait_ge(k_ready[u], k_ready.at(it, a + 1))
                        for h in range(HC):
                            q = slice(h * HD, (h + 1) * HD)
                            cp = nc.vector.tensor_copy(kblk[u][q, :, :, h, :],
                                                       kT[u][q].rearrange("p c (g n) -> p c g n", g=G))
                        cp.then_inc(kblk_ready[u], 1)
                    if step[:5] == "score" or step in ("exp0", "exp1", "exp2"):
                        L = int(step[-1])
                        k0 = (0, 4, 5)[L]
                        scale = (1.0, 1.0, float(HD) ** -0.5)[L]
                        ks = [part]

                        def views(k, L=L, u=u, b=b):
                            g, c = divmod(k, NC)
                            if L == 1:
                                return (b[2][:, 0:GN].rearrange("p (g n) -> p g n", g=G), absent[u][:],
                                        rmax[u][:, :, 0, 0], nmax[u][:, :, 0, 0], esum[u][:, :, 0, 0],
                                        rsum[u][:, :, 0, 0], G)
                            return (b[k][:, :].rearrange("p (h n) -> p h n", h=HC),
                                    absent[u][:, g:g + 1, :].to_broadcast([P, HC, P]),
                                    rmax[u][:, g, c], nmax[u][:, g, c], esum[u][:, g, c], rsum[u][:, g, c], HC)

                    if step[:5] == "score":
                        if L == 0 and part == 0:
                            dve.wait_ge(adj_ready[u], adj_ready.at(it, 1))
                        for k in ks:
                            s, m, mx, nm, _, _, n = views(k)
                            dve.wait_ge(s_ready[u], s_ready.at(it, k0 + k + 1))
                            if L == 0:
                                nc.vector.memset(mx, 0.0)
                                link(nc.vector.copy_predicated(s, m, fill[:].unsqueeze(2).to_broadcast([P, n, P])))
                            link(nc.vector.tensor_reduce(mx, s, AX_X, ALU.max))
                            nc.vector.tensor_scalar(nm, mx, -2.0 if L == 2 else -1.0, scale / 2 if L == 2 else 1.0,
                                                    ALU.mult, ALU.mult).then_inc(max_ready[u], 1)
                    if step in ("exp0", "exp1", "exp2"):
                        for k in ks:
                            _, _, _, _, es, rs, _ = views(k)
                            dve.wait_ge(exp_ready[u], exp_ready.at(it, k0 + k + 1))
                            nc.vector.reciprocal(rs, es).then_inc(r_ready[u], 1)
                    if step[:3] == "hop":
                        t = int(step[3])
                        for g in [part]:
                            dve.wait_ge(o_t[u], o_t.at(it, G * t + g + 1))
                            o = b[g][:, 0:D].rearrange("p (c n) -> p c n", c=NC)
                            z = zT[u][:, :, g * P:(g + 1) * P]
                            if t < HOPS:
                                a = nc.vector.scalar_tensor_tensor(z, vT[u][:, :, g * P:(g + 1) * P], ALPHA, o,
                                                                   ALU.mult, ALU.add)
                            else:
                                a = nc.vector.tensor_copy(z, o)
                            a.then_inc(zt_ready[u], 1)
                    if step in ("back3", "back4"):
                            t = int(step[4])
                            if t == HOPS and part == 0:
                                dve.wait_ge(xn_ready[u], xn_ready.at(it, 2))
                            for g in [part]:
                                dve.wait_ge(back[u], back.at(it, (G * t if t < HOPS else G * t + 1) + g + 1))
                                res = x_in[u] if t < HOPS else xnat[u]
                                a = nc.vector.tensor_tensor(y[u][:, g, :], b[2 + g][:, 0:D], res[:, g, :], ALU.add)
                            if part == G - 1:
                                link(a)
                    if step == "y1":
                        dve.wait_ge(xn_ready[u], xn_ready.at(it, 1))
                        dve.wait_ge(back[u], back.at(it, 9))
                        link(nc.vector.tensor_tensor(flat(y[u]), b[0][:, :], flat(xnat[u]), ALU.add))
                    if step in ("stat1", "stat2", "stat3"):
                        statistics(u, [y[u][:, g, :] for g in range(G)])
                    if step in ("nrm1", "nrm2", "nrm3"):
                        normalise(u, [y[u][:, g, :] for g in range(G)], int(step[-1]))
                    if step[:5] == "split":
                        dve.wait_ge(xt32[u], xt32.at(it, int(step[-1])))
                        nc.vector.tensor_tensor(flat(xT_lo[u]), flat(xT[u]), flat(xT_hi[u]).bitcast(F32),
                                                ALU.subtract).then_inc(xt_ready[u], 1)
                    if step == "mask":
                        for d in range(LABELS):
                            a = nc.vector.tensor_scalar(E[u][:, :, 0, d], adj_f[u][:], float(d + 1), None,
                                                        ALU.is_equal)
                        link(a)
                        for g in range(G):
                            a = nc.vector.tensor_reduce(cnt[u][:, g], E[u][:, g, 0], AX_X, ALU.add)
                        link(a)
                        link(nc.vector.tensor_scalar(cnt[u][:], cnt[u][:], DEG_EPS, None, ALU.add))
                        nc.vector.reciprocal(rcnt[u][:], cnt[u][:]).then_inc(wm_cnt[u], 1)
                    if step == "osplit":
                        dve.wait_ge(out32[u], out32.at(it, 1))
                        link(nc.vector.tensor_copy(flat(oT_hi[u]), flat(qT[u])))
                        nc.vector.tensor_tensor(flat(oT_lo[u]), flat(qT[u]), flat(oT_hi[u]).bitcast(F32),
                                                ALU.subtract).then_inc(out_ready[u], 1)
                    if step == "gate" and part == 0:
                        dve.wait_ge(gate_ready[u], gate_ready.at(it, 1))
                        link(nc.vector.tensor_scalar(rT[u][:], rT[u][:], 0.5, 0.5, ALU.mult, ALU.add))
                        for c in range(NC):
                            a = nc.vector.scalar_tensor_tensor(vnat[u][:, c, :], b[3][:, c * GN:(c + 1) * GN],
                                                               colc("bnh", c), rT[u][:, c, :], ALU.add, ALU.mult)
                        link(a)
                    if step == "gate" and part == 1:
                        dve.wait_ge(gates[u], gates.at(it, 2))
                        nc.vector.tensor_tensor(flat(vnat[u]), b[0][:, :], flat(vnat[u]), ALU.add)\
                            .then_inc(r_used[u], 1)
                    if step == "mix" and part == 0:
                        dve.wait_ge(gate_ready[u], gate_ready.at(it, 2))
                        link(nc.vector.tensor_tensor(flat(qT[u]), flat(xT[u]), flat(vnat[u]), ALU.subtract))
                    if step == "mix" and part == 1:
                        dve.wait_ge(gate_ready[u], gate_ready.at(it, 3))
                        link(nc.vector.scalar_tensor_tensor(flat(qT[u]), flat(vT[u]), 1.0, flat(qT[u]),
                                                            ALU.add, ALU.mult))
                        nc.vector.scalar_tensor_tensor(flat(qT[u]), flat(qT[u]), 0.5, flat(vnat[u]),
                                                       ALU.mult, ALU.add).then_inc(mixed[u], 1)
                    if step == "stat4":
                        dve.wait_ge(mixed_t[u], mixed_t.at(it, 1))
                        statistics(u, [b[1][:, g * D:(g + 1) * D] for g in range(G)])
                    if step == "last":
                        normalise(u, [b[1][:, g * D:(g + 1) * D] for g in range(G)], 4)
                        nc.vector.memset(var[u][:], 0.0).then_inc(bank1_free[u], 1)
            assert own.used == [DVE_OWN] * UNITS, own.used


_OUTS = [((GRAPHS, P, D), "float32")]


def kernel(**inputs):
    import concourse.bacc as _bacc
    from concourse.bass_utils import run_bass_kernel_spmd as _run

    def chunked(w):
        return np.asarray(w).reshape(-1, P, D).transpose(1, 0, 2)

    v = {k: np.asarray(a) for k, a in inputs.items()}
    w = [v[f"L0_gnn_W{n}"].T for n in "qkv"] + [v[f"L2_gnn_W{n}"] for n in "qkv"]
    w += [v["L3_gnn_Wd"].T[D * d:D * d + D] for d in range(LABELS)]
    w += [v[f"L3_gnn_W{n}"].T for n in ("ri", "zi", "ni", "rh", "zh", "nh")]
    l1 = [v["L1_gnn_Wq"].T, v["L1_gnn_Wk"].T, v["L1_gnn_Wv"].T, v["L1_gnn_Wo"]]
    vec = {f"b{n}{L}": v[f"L{L}_gnn_b{n}"] for L in (0, 2) for n in "qkv"}
    vec.update({f"b{n}": v[f"L3_gnn_b{n}"] for n in ("d", "ri", "rh", "zi", "zh", "ni", "nh")})
    vec.update({f"{n}{L}": v[f"L{L}_gnn_{n}"] for L in range(4) for n in ("gamma", "beta")})
    vec.update({f"bo{L}": v[f"L{L}_gnn_bo"] for L in (1, 2)})
    arrays = {
        "x": v["x"],
        "xt": v["x"].transpose(0, 2, 1),
        "adj": v["adj"],
        "weights": np.stack([chunked(a) for a in w], axis=1),
        "l1_weights": np.stack([chunked(a) for a in l1], axis=1),
        "wo2": chunked(v["L2_gnn_Wo"]),
        "cols": np.stack([vec[n].reshape(NC, P) for n in COLS]).reshape(-1, P).T,
        "rows": np.stack([vec[n] for n in ROWS]),
    }
    arrays = {f"in_{k}": np.ascontiguousarray(a) for k, a in arrays.items()}
    nc = _bacc.Bacc("TRN2", target_bir_lowering=False, num_devices=1)
    args = [nc.dram_tensor(n, a.shape, mybir.dt.from_np(a.dtype), kind="ExternalInput").ap()
            for n, a in arrays.items()]
    args += [nc.dram_tensor(f"out_{i}", shape, mybir.dt.from_np(np.dtype(dt)), kind="ExternalOutput").ap()
             for i, (shape, dt) in enumerate(_OUTS)]
    gnn_program(nc, *args)
    r = _run(nc, [arrays], core_ids=[0])
    return r.results[0]["out_0"]
```
